# Optimizing a Trainium2 kernel written in Bass

```python
import numpy as np
import jax
import jax.numpy as jnp

def _softmax(x, axis=-1):
    return jax.nn.softmax(x, axis=axis)

def _gelu(x):
    return jax.nn.gelu(x, approximate=True)

def _silu(x):
    return jax.nn.silu(x)

def _sigmoid(x):
    return jax.nn.sigmoid(x)

def _layernorm(x, axis=-1, eps=1e-05):
    m = jnp.mean(x, axis=axis, keepdims=True)
    v = jnp.var(x, axis=axis, keepdims=True)
    return (x - m) / jnp.sqrt(v + eps)

def _scatter_add(tgt, idx, src, axis=0):
    return tgt.at[idx].add(src)

def _segment_sum(src, seg, n):
    return jax.ops.segment_sum(src, seg, n)
kernel_name = 'mk_seq_preln_d1_jaxref_r8_77fbf1'

def setup_inputs(seed: int=0):
    np.random.seed(seed)
    _w = jnp.asarray

    def _L0_attn_setup():
        import jax, jax.numpy as jnp
        import numpy as np
        N_HEADS = 16
        key = jax.random.key(seed)
        ks = jax.random.split(key, 9)
        B, S, D = (2, 256, 256)
        s = 0.02
        return {'X': jax.random.normal(ks[0], (B, S, D), jnp.float32), 'Wq': jax.random.normal(ks[1], (D, D), jnp.float32) * s, 'bq': jax.random.normal(ks[2], (D,), jnp.float32) * s, 'Wk': jax.random.normal(ks[3], (D, D), jnp.float32) * s, 'bk': jax.random.normal(ks[4], (D,), jnp.float32) * s, 'Wv': jax.random.normal(ks[5], (D, D), jnp.float32) * s, 'bv': jax.random.normal(ks[6], (D,), jnp.float32) * s, 'Wo': jax.random.normal(ks[7], (D, D), jnp.float32) * s, 'bo': jax.random.normal(ks[8], (D,), jnp.float32) * s}
    _L0_attn_in = _L0_attn_setup()

    def _L0_ffn_setup():
        import jax, jax.numpy as jnp
        import numpy as np
        K_TOP = 2
        key = jax.random.key(seed)
        k0, k1, k2 = jax.random.split(key, 3)
        B, S, D, E, F = (4, 256, 256, 8, 256)
        x = jax.random.normal(k0, (B, S, D), dtype=jnp.float32)
        Wr = jax.random.normal(k1, (D, E), dtype=jnp.float32) * 0.02
        We = jax.random.normal(k2, (E, D, F), dtype=jnp.float32) * 0.02
        be = jnp.zeros((E, F), dtype=jnp.float32)
        return {'x': x, 'Wr': Wr, 'We': We, 'be': be}
    _L0_ffn_in = _L0_ffn_setup()
    _d = {'L0_attn_X': _L0_attn_in['X'], 'L0_attn_Wq': _L0_attn_in['Wq'], 'L0_attn_bq': _L0_attn_in['bq'], 'L0_attn_Wk': _L0_attn_in['Wk'], 'L0_attn_bk': _L0_attn_in['bk'], 'L0_attn_Wv': _L0_attn_in['Wv'], 'L0_attn_bv': _L0_attn_in['bv'], 'L0_attn_Wo': _L0_attn_in['Wo'], 'L0_attn_bo': _L0_attn_in['bo'], 'L0_ffn_Wr': _L0_ffn_in['Wr'], 'L0_ffn_We': _L0_ffn_in['We'], 'L0_ffn_be': _L0_ffn_in['be']}
    _x0 = _d['L0_attn_X']
    _d['L0_attn_X'] = jax.random.normal(jax.random.fold_in(jax.random.key(seed), 1), (1, 2048, 256), dtype=_x0.dtype)
    del _x0
    return _d

def reference(L0_attn_X, L0_attn_Wq, L0_attn_bq, L0_attn_Wk, L0_attn_bk, L0_attn_Wv, L0_attn_bv, L0_attn_Wo, L0_attn_bo, L0_ffn_Wr, L0_ffn_We, L0_ffn_be):

    def _L0_attn_ref(X, Wq, bq, Wk, bk, Wv, bv, Wo, bo):
        import jax, jax.numpy as jnp
        import numpy as np
        N_HEADS = 16
        B, S, D = X.shape
        H = N_HEADS
        d_head = D // H
        scale = jnp.asarray(1.0 / np.sqrt(np.sqrt(d_head)), X.dtype)
        Q = (X @ Wq.T + bq).reshape(B, S, H, d_head) * scale
        K = (X @ Wk.T + bk).reshape(B, S, H, d_head) * scale
        V = (X @ Wv.T + bv).reshape(B, S, H, d_head)
        scores = jnp.einsum('bqhd,bkhd->bhqk', Q, K)
        causal = jnp.tril(jnp.ones((S, S), bool))
        scores = jnp.where(causal[None, None], scores, -jnp.inf)
        attn = jax.nn.softmax(scores.astype(jnp.float32), axis=-1).astype(X.dtype)
        out = jnp.einsum('bhqk,bkhd->bqhd', attn, V).reshape(B, S, D)
        return out @ Wo.T + bo

    def _L0_ffn_ref(x, Wr, We, be):
        import jax, jax.numpy as jnp
        import numpy as np
        K_TOP = 2
        logits = jnp.einsum('bsd,de->bse', x, Wr)
        w, sel = jax.lax.top_k(logits, K_TOP)
        w = jax.nn.softmax(w, axis=-1)
        E = We.shape[0]
        gate = jnp.einsum('bsk,bske->bse', w, jax.nn.one_hot(sel, E, dtype=w.dtype))
        out = jnp.zeros(x.shape[:2] + (We.shape[2],), dtype=x.dtype)
        for e in range(E):
            out = out + gate[..., e:e + 1] * (jnp.einsum('bsd,df->bsf', x, We[e]) + be[e])
        return out
    x = L0_attn_X
    x = x + _L0_attn_ref(_layernorm(x, axis=-1), L0_attn_Wq, L0_attn_bq, L0_attn_Wk, L0_attn_bk, L0_attn_Wv, L0_attn_bv, L0_attn_Wo, L0_attn_bo)
    x = x + _L0_ffn_ref(_layernorm(x, axis=-1), L0_ffn_Wr, L0_ffn_We, L0_ffn_be)
    return x

_drawn_inputs = setup_inputs


def setup_inputs(seed=0):
    import zlib

    import numpy as np

    out = dict(_drawn_inputs(seed))
    spreads = {'L0_ffn_be': (0.0, 0.1)}
    factors = {'L0_attn_Wq': 8.0,
     'L0_attn_bq': 8.0,
     'L0_attn_Wk': 8.0,
     'L0_attn_bk': 8.0,
     'L0_attn_Wv': 4.347,
     'L0_attn_bv': 2.722}
    for name, (base, spread) in spreads.items():
        noise = np.random.default_rng([zlib.crc32(name.encode()), seed]).standard_normal(out[name].shape)
        drawn = base * np.exp(spread * noise) if base else spread * noise
        out[name] = jnp.asarray(drawn.astype(out[name].dtype))
    for name, factor in factors.items():
        out[name] = (out[name] * factor).astype(out[name].dtype)
    return out
```

```python
from contextlib import ExitStack

import concourse.bass as bass
from concourse import mybir
from concourse.alu_op_type import AluOpType as ALU

F32 = mybir.dt.float32
BF16 = mybir.dt.bfloat16
U32 = mybir.dt.uint32
ACT = mybir.ActivationFunctionType
AX = mybir.AxisListType

P = 128
S = 2048
D = 256
H = 16
DH = D // H
E = 8
F = 256
EPS = 1e-5
NEG = -1e30

FC = D // P
NT = S // P
CW = 512
NC = S // CW
TC = CW // P
HG = 4
NG = H // HG
Q_PARTS = (0, 0, 0, 1, 1, 2)
K_PARTS = (0, 1, 2, 0, 1, 0)
TERMS = len(Q_PARTS)
SR = TERMS * DH
SX = SR + 3
VW = 32

M_RING = 3
M_LAG = 12


def max_stream():
    out = []
    for c in range(NC):
        blocks = [("max", c, t, j, kc) for t in range(TC) for j in range(HG) for kc in range(c + 1)]
        out += blocks[:M_LAG] + [("turn", (c - 1) % NC)] + blocks[M_LAG:]
    return out


STREAM = max_stream()
SN = len(STREAM)
M_END = [max(i for i, m in enumerate(STREAM) if m[0] == "max" and m[1] == c) for c in range(NC)]
LEAD = 92


def m_free(i):
    return M_RING if i >= SN % M_RING else SN % M_RING


def m_width(m):
    if m[0] == "turn":
        return P
    _, c, t, _, kc = m
    return CW if kc < c else (t + 1) * P


STEPS = [(c, kt) for c in range(NC) for kt in range(TC * (c + 1))]
SS = len(STEPS)
C_END = [max(s for s, (c, _) in enumerate(STEPS) if c == cc) for cc in range(NC)]
PV_LAG = 2
P_SLOTS = 4
DIAGS = NC * TC


def diag(s):
    c, kt = STEPS[s]
    return kt - TC * c if kt >= TC * c else None


def step_off(s):
    return P * (diag(s) or 0)


def body_stream():
    order = [(i, False) for i in range(LEAD, SN)] + [(i, True) for i in range(LEAD)]
    m_total = sum(m_width(m) for m in STREAM)
    s_total = sum(CW - step_off(s) for s in range(SS))
    out, at, m_cols, s_cols = [], 0, 0, 0
    for s in range(SS):
        s_cols += CW - step_off(s)
        mine = []
        while at < SN and (m_cols < m_total * s_cols / s_total or s == SS - 1):
            mine.append(order[at])
            m_cols += m_width(STREAM[order[at][0]])
            at += 1
        out.append(mine)
    return out


BODY = body_stream()


def stream_place(i, following):
    return SN - LEAD + i if following else i - LEAD


TURNS_BEFORE = sum(m[0] == "turn" for m in STREAM[1 + M_LAG:LEAD])


def turn_number(place):
    return 1 + TURNS_BEFORE + sum(m[0] == "turn" for m in (STREAM[LEAD:] + STREAM[:LEAD])[:place])


def build_program(nc, X, WqT, WkT, WvT, WoT, bq, bk, bv, bo, Wr, We, be, ident, trimask, out):
    ctx = ExitStack()
    with ctx:
        def sb(name, shape, dt=F32):
            return ctx.enter_context(nc.sbuf_tensor(name, shape, dt))

        def sem(name):
            return ctx.enter_context(nc.semaphore(name))

        qk_d = nc.dram_tensor("qk_parts", [2, 3, D, S], BF16, kind="Internal").ap()
        num_d = nc.dram_tensor("attn_num", [D, S], F32, kind="Internal").ap()
        den_d = nc.dram_tensor("attn_den", [H, S], F32, kind="Internal").ap()
        rden_d = nc.dram_tensor("attn_rden", [H, S], F32, kind="Internal").ap()

        x_sb = sb("x_sb", [P, NT, D])
        wq, wk, wv, wo = (sb(n, [P, FC, D]) for n in ("wq", "wk", "wv", "wo"))
        we_sb = sb("we_sb", [P, FC, E * F])
        wr_sb = sb("wr_sb", [P, FC, E])
        be_sb = sb("be_sb", [E, F])
        bv_sb = sb("bv_sb", [P, D])
        bo_sb = sb("bo_sb", [P, D])
        bqk = sb("bqk", [P, 2, FC])
        bqk_half = sb("bqk_half", [P, 2, FC])
        id_f = sb("id_f", [P, P])
        id_b = sb("id_b", [P, P], BF16)
        tri = sb("tri", [P, CW])
        iota = sb("iota", [P, E])
        parts = sb("parts", [P, 2, 3, CW], BF16)
        V = sb("V", [P, NT, D])
        Vg = [sb(f"Vg{b}", [P, NT, HG, VW]) for b in range(2)]
        Qo = [sb(f"Qo{b}", [P, NC, HG, CW], BF16) for b in range(2)]
        Ko = [sb(f"Ko{b}", [P, HG, S], BF16) for b in range(2)]
        probs = sb("probs", [P, P_SLOTS, HG, CW])
        O_sb = sb("O_sb", [P, 2, CW])
        junk = sb("junk", [P, M_RING, CW], BF16)
        pm = sb("pm", [P, NC, HG * TC, NC])
        mx = sb("mx", [P, HG * TC])
        mr = sb("mr", [P, HG * TC])
        mparts = sb("mparts", [P, 2, 5, HG * TC], BF16)
        mT = sb("mT", [3 * HG * TC, 2, P], BF16)
        st6 = sb("st6", [P, TC, 6])
        mv = sb("mv", [P, TC, 2])
        ve = sb("ve", [P, TC])
        rs = sb("rs", [P, TC])
        ta = sb("ta", [P, TC])
        neg_half = sb("neg_half", [P, TC])
        tb = sb("tb", [P, TC])
        den_c = sb("den_c", [P, H * S // P])
        rden_c = sb("rden_c", [P, H * S // P])
        lg = sb("lg", [P, TC, E])
        top = sb("top", [P, TC, 8])
        idx = sb("idx", [P, TC, 8], U32)
        idf = sb("idf", [P, TC, 2])
        gd = sb("gd", [P, TC])
        ge = sb("ge", [P, TC])
        gs = sb("gs", [P, TC])
        gw = sb("gw", [P, TC, 2])
        g1 = sb("g1", [P, TC, E])
        g2 = sb("g2", [P, TC, E])
        gT = sb("gT", [E, CW])
        gates = sb("gates", [P, 2, TC, E])

        q1f = Qo[1][:, :, :, :].rearrange("p c j w -> p (c j w)").bitcast(F32)
        xT = Ko[1][:, :, :].rearrange("p j s -> p (j s)").bitcast(F32).rearrange("p (f s) -> p f s", f=FC)
        xh = q1f[:, 0:2 * TC * D].rearrange("p (b t d) -> p b t d", b=2, t=TC)
        qf = q1f[:, 2048:3072].rearrange("p (b w) -> p b w", b=2)
        r1 = q1f[:, 3072:4096].rearrange("p (b w) -> p b w", b=2)
        pr = probs[:, :, :, :].rearrange("p a j w -> p (a j w)")
        nm = pr[:, 0:2048].rearrange("p (b f w) -> p b f w", b=2, f=FC)
        rd = pr[:, 2048:4096].rearrange("p (b f w) -> p b f w", b=2, f=FC)
        at = pr[:, 4096:5120].rearrange("p (f w) -> p f w", f=FC)
        xh2 = pr[:, 5120:6144].rearrange("p (t d) -> p t d", t=TC)
        xT2 = pr[:, 6144:8192].rearrange("p (b f w) -> p b f w", b=2, f=FC)
        yb = V[:, 0:2 * TC, :].rearrange("p (b t) d -> p b t d", b=2)

        ST = [ctx.enter_context(nc.psum_tensor(f"ST{i}", [P, 2, CW], F32)) for i in range(2)]
        MB = [ctx.enter_context(nc.psum_tensor(f"MB{i}", [P, CW], F32)) for i in range(M_RING)]
        OB = ctx.enter_context(nc.psum_tensor("OB", [P, CW], F32))
        PB = [OB, MB[2]]
        ring4 = [ST[0][:, 0, :], ST[0][:, 1, :], ST[1][:, 0, :], ST[1][:, 1, :]]

        x_loaded = [sem(f"x_loaded{c}") for c in range(NC)]
        w_loaded, v_loaded, e_loaded = sem("w_loaded"), sem("v_loaded"), sem("e_loaded")
        consts_ready = sem("consts_ready")
        var_ready, rsqrt_ready = sem("var_ready"), sem("rsqrt_ready")
        ln_step = sem("ln_step")
        xh_ready = sem("xh_ready")
        pro_ready, pro_done = sem("pro_ready"), sem("pro_done")
        bias_ready = sem("bias_ready")
        qf_ready, high_ready, rest_ready, mid_ready, low_ready = (
            sem(n) for n in ("qf_ready", "high_ready", "rest_ready", "mid_ready", "low_ready"))
        parts_stored = [sem(f"parts_stored{i}") for i in range(2)]
        v_biased = sem("v_biased")
        vg_set, vg_ready = sem("vg_set"), sem("vg_ready")
        ones_ready, ones_copied = sem("ones_ready"), sem("ones_copied")
        xb_ready = sem("xb_ready")
        first_ops = [sem(f"first_ops{c}") for c in range(NC)]
        ops_loaded = [sem(f"ops_loaded{b}") for b in range(2)]
        m_ready, m_done = sem("m_ready"), sem("m_done")
        folded = sem("folded")
        mpost_step = sem("mpost_step")
        mparts_ready = sem("mparts_ready")
        mrow = [sem(f"mrow{i}") for i in range(2)]
        st_ready, exp_done = sem("st_ready"), sem("exp_done")
        mask_done, pv_done = sem("mask_done"), sem("pv_done")
        o_out = sem("o_out")
        o_stored = [sem(f"o_stored{i}") for i in range(2)]
        den_loaded, rden_ready, rden_stored = sem("den_loaded"), sem("rden_ready"), sem("rden_stored")
        at_loaded = [sem(f"at_loaded{i}") for i in range(2)]
        at_ready, wo_ready, x1_ready = sem("at_ready"), sem("wo_ready"), sem("x1_ready")
        xh2_ready, xt2_psum, xt2_ready = sem("xh2_ready"), sem("xt2_psum"), sem("xt2_ready")
        lg_ready, gd_ready, ge_ready, gates_ready = sem("lg_ready"), sem("gd_ready"), sem("ge_ready"), sem("gates_ready")
        lg_read = sem("lg_read")
        ex_ready, ex_done = sem("ex_ready"), sem("ex_done")
        gt_psum, gt_ready, gb_ready, yb_ready = sem("gt_psum"), sem("gt_ready"), sem("gb_ready"), sem("yb_ready")
        y_stored = [sem(f"y_stored{i}") for i in range(2)]
        dve_passed, pool_passed, sp_passed = sem("dve_passed"), sem("pool_passed"), sem("sp_passed")

        PRO_F1 = 4 * NC
        TURN0 = SN - LEAD

        def phase1_order():
            out = [("T", 0, 0), ("T", 0, 1)]
            for c in range(NC):
                if c + 1 < NC:
                    out += [("T", c + 1, 0), ("T", c + 1, 1)]
                out += [("QK", c, 0, 0), ("QK", c, 0, 1)]
            return out

        PHASE2 = [("V", i) for i in range(NT // 2)] + [("QK", c, 1, s) for c in range(NC) for s in range(2)]
        PRO = phase1_order() + PHASE2
        M_CHUNK_START = [0] + [e + 1 for e in M_END[:-1]]

        block = ctx.enter_context(nc.Block())

        @block.sync
        def _(sp):
            xv = X.rearrange("(c t p) d -> c p t d", t=TC, p=P)

            def load_x(c):
                sp.dma_start(x_sb[:, TC * c:TC * (c + 1), :], xv[c]).then_inc(x_loaded[c], 16)

            for i in range(2):
                sp.sem_inc(o_stored[i], 16)
            load_x(0)
            sp.dma_start(id_f[:, :], ident).then_inc(w_loaded, 16)
            sp.dma_start(wq[:, :, :], WqT.rearrange("(a p) n -> p a n", p=P)).then_inc(w_loaded, 16)
            sp.dma_start(wk[:, :, :], WkT.rearrange("(a p) n -> p a n", p=P)).then_inc(w_loaded, 16)
            for side, b in enumerate((bq, bk)):
                sp.dma_start(bqk[:, side, :], b.rearrange("(a p) -> p a", p=P),
                             allow_slow_non_contiguous=True).then_inc(w_loaded, 16)
            for c in range(1, NC):
                load_x(c)
            sp.dma_start(tri[:, :], trimask).then_inc(v_loaded, 16)
            sp.dma_start(wv[:, :, :], WvT.rearrange("(a p) n -> p a n", p=P)).then_inc(v_loaded, 16)
            sp.dma_start(bv_sb[:, :], bv.partition_broadcast(P)).then_inc(v_loaded, 16)
            sp.dma_start(bo_sb[:, :], bo.partition_broadcast(P)).then_inc(v_loaded, 16)

            def store_parts(v, c, f, side):
                sp.wait_ge(low_ready, v + 1)
                dst = qk_d[side, :, P * f:P * (f + 1), CW * c:CW * (c + 1)].rearrange("a f q -> f a q")
                sp.dma_start(dst, parts[:, v % 2, :, :]).then_inc(parts_stored[v % 2], 16)

            for c in range(NC):
                for side in range(2):
                    store_parts(2 * c + side, c, 0, side)
                sp.wait_ge(parts_stored[0], 16 * (c + 1))
                sp.wait_ge(parts_stored[1], 16 * (c + 1))
                for n in range(TERMS):
                    rows = slice(DH * n, DH * (n + 1))
                    cols = slice(CW * c, CW * (c + 1))
                    sp.dma_start(Qo[0][rows, c, :, :], qk_d[0, Q_PARTS[n], 0:HG * DH, cols]
                                 .rearrange("(j d) q -> d j q", d=DH)).then_inc(first_ops[c], 16)
                    sp.dma_start(Ko[0][rows, :, cols], qk_d[1, K_PARTS[n], 0:HG * DH, cols]
                                 .rearrange("(j d) q -> d j q", d=DH)).then_inc(first_ops[c], 16)

            def load_group(b, row):
                for n in range(TERMS):
                    rows = slice(DH * n, DH * (n + 1))
                    for c in range(NC):
                        src = qk_d[0, Q_PARTS[n], bass.ds(row, HG * DH), CW * c:CW * (c + 1)]
                        sp.dma_start(Qo[b][rows, c, :, :], src.rearrange("(j d) q -> d j q", d=DH))\
                          .then_inc(ops_loaded[b], 16)
                    src = qk_d[1, K_PARTS[n], bass.ds(row, HG * DH), :]
                    sp.dma_start(Ko[b][rows, :, :], src.rearrange("(j d) q -> d j q", d=DH))\
                      .then_inc(ops_loaded[b], 16)

            def place_row(b, c, slot, m_seen):
                sp.wait_ge(m_done, m_seen)
                for n in range(3):
                    sp.dma_start(Qo[b][SR + n:SR + n + 1, c, :, :], mT[HG * TC * n:HG * TC * (n + 1), slot, :])\
                      .then_inc(mrow[slot], 16)

            turn_at = {i: m[1] for i, m in enumerate(STREAM[:LEAD]) if m[0] == "turn" and i > M_LAG}
            turns = sorted(turn_at.items())
            v = 2 * NC
            for c in range(NC):
                for side in range(2):
                    store_parts(v, c, 1, side)
                    v += 1
                if c < len(turns):
                    i, ch = turns[c]
                    place_row(0, ch, (ch + 1) % 2, i + 1)
            sp.dma_start(wo[:, :, :], WoT.rearrange("(a p) n -> p a n", p=P)).then_inc(e_loaded, 16)
            sp.dma_start(wr_sb[:, :, :], Wr.rearrange("(a p) e -> p a e", p=P)).then_inc(e_loaded, 16)
            for e in range(E):
                sp.dma_start(we_sb[:, :, F * e:F * (e + 1)], We[e].rearrange("(a p) f -> p a f", p=P))\
                  .then_inc(e_loaded, 16)
            sp.dma_start(be_sb[:, :], be).then_inc(e_loaded, 16)
            sp.wait_ge(parts_stored[0], 16 * 2 * NC)
            sp.wait_ge(parts_stored[1], 16 * 2 * NC)

            sp.wait_ge(st_ready, 1)
            sp.wait_ge(ones_ready, 1)
            sp.dma_start(Ko[1][SR:SX, :, :], Ko[0][SR:SX, :, :]).then_inc(ones_copied, 16)

            with sp.Fori(0, NG // 2) as it:
                for u in range(2):
                    m_base = LEAD + SN * (2 * it + u)
                    sp.wait_ge(st_ready, (2 * it + u) * (2 * SS) + 1)
                    sp.sem_inc(sp_passed, 1)
                    load_group(1 - u, (2 * it + 1) * (HG * DH) if u == 0 else (1 - it) * (2 * HG * DH))
                    for s in range(SS):
                        for i, following in BODY[s]:
                            if STREAM[i][0] == "turn":
                                c = STREAM[i][1]
                                b = 1 - u if following and i > M_LAG else u
                                place_row(b, c, (c + 1) % 2, m_base + (stream_place(i, following) + 1))
                        for c in range(NC):
                            if s == min(C_END[c] + PV_LAG + 1, SS - 1):
                                sp.wait_ge(o_out, (2 * it + u) * NC + (c + 2))
                                for j in range(HG):
                                    cols = slice(CW * c, CW * (c + 1))
                                    head = it * (2 * HG) + (u * HG + j)
                                    sp.dma_start(num_d[bass.ds(head * DH, DH), cols],
                                                 O_sb[32 * j:32 * j + DH, c % 2, :]).then_inc(o_stored[c % 2], 16)
                                    sp.dma_start(den_d[bass.ds(head, 1), cols],
                                                 O_sb[32 * j + DH:32 * j + DH + 1, c % 2, :])\
                                      .then_inc(o_stored[c % 2], 16)

            for i in range(2):
                sp.wait_ge(o_stored[i], 16 + 16 * 2 * HG * (NG * NC // 2))
            flat = "h (a w) -> (h a) w"
            sp.dma_start(den_c[:, :], den_d.rearrange(flat, w=H * S // P)).then_inc(den_loaded, 16)

            def load_num(c):
                for f in range(FC):
                    sp.dma_start(nm[:, c % 2, f, :], num_d[P * f:P * (f + 1), CW * c:CW * (c + 1)])\
                      .then_inc(at_loaded[c % 2], 16)

            def load_rden(c):
                for f in range(FC):
                    hs = P // DH
                    src = rden_d[hs * f:hs * (f + 1), CW * c:CW * (c + 1)]
                    sp.dma_start(rd[:, c % 2, f, :], src.unsqueeze(1).broadcast_to([hs, DH, CW]))\
                      .then_inc(at_loaded[c % 2], 16)

            sp.wait_ge(pv_done, P_SLOTS + NG * SS)
            load_num(0)
            load_num(1)
            sp.wait_ge(rden_ready, 1)
            sp.dma_start(rden_d.rearrange(flat, w=H * S // P), rden_c[:, :]).then_inc(rden_stored, 16)
            sp.wait_ge(rden_stored, 16)
            load_rden(0)
            load_rden(1)
            ov = out.rearrange("(n p) d -> n p d", p=P)
            for c in range(NC):
                if c + 2 < NC:
                    sp.wait_ge(at_ready, c + 1)
                    load_num(c + 2)
                    load_rden(c + 2)
                for t in range(TC):
                    sp.wait_ge(ex_done, (TC * c + t + 1) * (E // 2))
                    sp.dma_start(ov[TC * c + t], yb[:, c % 2, t, :]).then_inc(y_stored[c % 2], 16)
            for i in range(2):
                sp.wait_ge(y_stored[i], 16 * NT // 2)

        @block.tensor
        def _(pe):
            def stream_entry(i, b, n, turn):
                m = STREAM[i]
                if not (isinstance(n, int) and n < M_RING):
                    pe.wait_ge(m_done, n + 1 - m_free(i))
                bank = MB[i % M_RING]
                if m[0] == "turn":
                    if not (isinstance(turn, int) and turn == 0):
                        pe.wait_ge(mparts_ready, turn)
                    slot = (m[1] + 1) % 2
                    nc.tensor.transpose(bank[0:5 * HG * TC, 0:P // 2].bitcast(BF16),
                                        mparts[:, slot, :, :].rearrange("p a m -> p (a m)"), id_b[:, :])\
                      .then_inc(m_ready, 1)
                    return
                _, c, t, j, kc = m
                w = m_width(m)
                nc.tensor.matmul(bank[:, 0:w], Qo[b][0:SR, c, j, P * t:P * (t + 1)],
                                 Ko[b][0:SR, j, CW * kc:CW * kc + w], start=True, stop=True).then_inc(m_ready, 1)

            def pro_bank(n, item):
                if n >= 4:
                    pe.wait_ge(pro_done, n - 3)
                bank = ring4[n % 4]
                if item[0] == "T":
                    _, c, f = item
                    if f == 0:
                        pe.wait_ge(xh_ready, c + 1)
                    for t in range(TC):
                        last = nc.tensor.transpose(bank[:, P * t:P * (t + 1)], xh[:, c % 2, t, P * f:P * (f + 1)],
                                                   id_f[:, :])
                elif item[0] == "QK":
                    _, c, f, side = item
                    pe.wait_ge(pro_done, 1 + PRO.index(("T", c, 1)))
                    for a in range(FC):
                        last = nc.tensor.matmul(bank, (wq, wk)[side][:, a, P * f:P * (f + 1)],
                                                xT[:, a, CW * c:CW * (c + 1)], start=(a == 0), stop=(a == FC - 1))
                else:
                    if item[1] == 0:
                        pe.wait_ge(v_loaded, 64)
                    for t in range(2):
                        kt = 2 * item[1] + t
                        for a in range(FC):
                            last = nc.tensor.matmul(bank[:, D * t:D * (t + 1)], xT[:, a, P * kt:P * (kt + 1)],
                                                    wv[:, a, :], start=(a == 0), stop=(a == FC - 1))
                last.then_inc(pro_ready, 1)

            pe.sem_inc(pv_done, P_SLOTS)
            pe.wait_ge(w_loaded, 80)
            for n in range(PRO_F1):
                pro_bank(n, PRO[n])
            pe.wait_ge(consts_ready, 2)
            n = PRO_F1
            turns = 0
            for i in range(LEAD):
                for c in range(NC):
                    if i == M_CHUNK_START[c]:
                        pe.wait_ge(first_ops[c], 16 * 2 * TERMS)
                stream_entry(i, 0, i, turns)
                turns += STREAM[i][0] == "turn"
                while n < len(PRO) and (n - PRO_F1) * LEAD < (i + 1) * len(PHASE2):
                    pro_bank(n, PRO[n])
                    n += 1

            pe.wait_ge(pro_done, len(PRO))

            with pe.Fori(0, NG // 2) as it:
                for u in range(2):
                    g = 2 * it + u
                    m_base = LEAD + SN * g

                    def scores(s, j, u=u, g=g, it=it):
                        c, kt = STEPS[s]
                        w = CW - step_off(s)
                        if kt == 0 and j == 0:
                            slot = (c + 1) % 2
                            pe.wait_ge(mrow[slot], 48 * (2 * g + (c // 2 + 1)))
                        p = j // 2
                        if j % 2 == 0:
                            pe.wait_ge(exp_done, g * (2 * SS) + (2 * s + p + 1))
                        ins = nc.tensor.matmul(ST[p][:, j % 2, 0:w], Ko[u][0:SX, j, P * kt:P * (kt + 1)],
                                               Qo[u][0:SX, c, j, CW - w:CW], start=True, stop=True)
                        if j % 2:
                            ins.then_inc(st_ready, 1)

                    def values(s, u=u, g=g, it=it):
                        c, kt = STEPS[s]
                        w = CW - step_off(s)
                        if kt == 0:
                            pe.wait_ge(o_out, g * NC + (c + 1))
                        if diag(s) is None:
                            pe.wait_ge(exp_done, g * (2 * SS) + (2 * s + 2 + 2))
                        else:
                            pe.wait_ge(mask_done, g * DIAGS + (TC * c + diag(s) + 1))
                        for j in range(HG):
                            last = nc.tensor.matmul(
                                OB[32 * j:32 * j + VW, CW - w:CW], Vg[u][:, kt, j, :],
                                probs[:, s % P_SLOTS, j, 0:w], start=(kt == 0), stop=(kt == TC * (c + 1) - 1),
                                tile_position=(0, 32 * j))
                        last.then_inc(pv_done, 1)

                    pe.wait_ge(vg_ready, g + 1)
                    pe.wait_ge((ones_ready, ones_copied)[u], (1, 16)[u])
                    for s in range(SS):
                        between = [[] for _ in range(HG + 1)]
                        for k, entry in enumerate(BODY[s]):
                            between[(2 * k + 1) * (HG + 1) // (2 * len(BODY[s]))].append(entry)
                        for j in range(HG + 1):
                            if j < HG:
                                scores(s, j)
                            elif s >= PV_LAG:
                                values(s - PV_LAG)
                            for i, following in between[j]:
                                if following and i == 0:
                                    pe.wait_ge(ops_loaded[1 - u], (it + 1) * (16 * TERMS * (NC + 1)))
                                place = stream_place(i, following)
                                stream_entry(i, 1 - u if following else u, m_base + place,
                                             NC * g + turn_number(place))
                    for s in range(SS - PV_LAG, SS):
                        values(s)

            pe.wait_ge(e_loaded, 16 * (3 + E))

            def project(c):
                pe.wait_ge(at_ready, c + 1)
                for h in range(2):
                    if c == 0:
                        if h == 0:
                            pe.wait_ge(o_out, NG * NC + 1)
                        else:
                            pe.wait_ge(m_done, LEAD + SN * NG)
                    else:
                        pe.wait_ge(yb_ready, 2 * (c - 1) + h + 1)
                    for t in range(2):
                        tok = P * (2 * h + t)
                        for a in range(FC):
                            last = nc.tensor.matmul(PB[h][:, D * t:D * (t + 1)], at[:, a, tok:tok + P], wo[:, a, :],
                                                    start=(a == 0), stop=(a == FC - 1))
                    last.then_inc(wo_ready, 1)

            def turn(c):
                pe.wait_ge(xh2_ready, c + 1)
                for f in range(FC):
                    if c == 0:
                        pe.wait_ge(m_done, LEAD + SN * NG)
                    elif f == 0:
                        pe.wait_ge(lg_read, c)
                        pe.wait_ge(xt2_ready, 2 * c)
                    for t in range(TC):
                        last = nc.tensor.transpose(MB[f][:, P * t:P * (t + 1)], xh2[:, t, P * f:P * (f + 1)], id_f[:, :])
                    last.then_inc(xt2_psum, 1)

            def logits(c):
                pe.wait_ge(xt2_ready, 2 * (c + 1))
                for t in range(TC):
                    for a in range(FC):
                        last = nc.tensor.matmul(MB[0][:, E * t:E * (t + 1)], xT2[:, c % 2, a, P * t:P * (t + 1)],
                                                wr_sb[:, a, :], start=(a == 0), stop=(a == FC - 1))
                last.then_inc(lg_ready, 1)

            def experts(c, t):
                for e2 in range(E // 2):
                    n = (TC * c + t) * (E // 2) + e2
                    if n >= 4:
                        pe.wait_ge(ex_done, n - 3)
                    elif n == 0:
                        pe.wait_ge(exp_done, 2 + NG * SS * 2)
                    for a in range(FC):
                        last = nc.tensor.matmul(ring4[n % 4], xT2[:, c % 2, a, P * t:P * (t + 1)],
                                                we_sb[:, a, 2 * F * e2:2 * F * (e2 + 1)],
                                                start=(a == 0), stop=(a == FC - 1))
                    last.then_inc(ex_ready, 1)

            def gated_bias(c):
                pe.wait_ge(gates_ready, c + 1)
                for t in range(TC):
                    last = nc.tensor.transpose(MB[1][0:E, P * t:P * (t + 1)], gates[:, c % 2, t, :], id_f[:, :])
                last.then_inc(gt_psum, 1)
                pe.wait_ge(gt_ready, c + 1)
                for h in range(2):
                    for t in range(2):
                        tok = P * (2 * h + t)
                        last = nc.tensor.matmul(PB[h][:, D * t:D * (t + 1)], gT[:, tok:tok + P], be_sb[:, :],
                                                start=True, stop=True)
                    last.then_inc(gb_ready, 1)

            project(0)
            turn(0)
            logits(0)
            for c in range(NC):
                more = c + 1 < NC
                experts(c, 0)
                gated_bias(c)
                experts(c, 1)
                if more:
                    project(c + 1)
                experts(c, 2)
                if more:
                    turn(c + 1)
                experts(c, 3)
                if more:
                    logits(c + 1)

        @block.scalar
        def _(act):
            act.sem_inc(exp_done, 2)
            act.sem_inc(o_out, 1)
            act.wait_ge(bias_ready, 1)
            v = 0
            pending = None

            def middle(v):
                act.wait_ge(rest_ready, v + 1)
                nc.scalar.activation(parts[:, v % 2, 1, :], r1[:, v % 2, :], ACT.Copy).then_inc(mid_ready, 1)

            for n, item in enumerate(PRO):
                act.wait_ge(pro_ready, n + 1)
                bank = ring4[n % 4]
                if item[0] == "T":
                    _, c, f = item
                    nc.scalar.activation(xT[:, f, CW * c:CW * (c + 1)], bank, ACT.Copy).then_inc(pro_done, 1)
                elif item[0] == "V":
                    kt = 2 * item[1]
                    nc.scalar.activation(V[:, kt:kt + 2, :].rearrange("p t d -> p (t d)"), bank, ACT.Copy)\
                      .then_inc(pro_done, 1)
                else:
                    _, c, f, side = item
                    if v >= 2:
                        act.wait_ge(rest_ready, v - 1)
                        act.wait_ge(parts_stored[v % 2], 16 * (v // 2))
                    nc.scalar.activation(qf[:, v % 2, :], bank, ACT.Identity, bias=bqk_half[:, side, f:f + 1],
                                         scale=0.5).then_inc(pro_done, 1)
                    act.wait_ge(pro_done, n + 1)
                    nc.scalar.activation(parts[:, v % 2, 0, :], qf[:, v % 2, :], ACT.Copy).then_inc(high_ready, 1)
                    if v % 2:
                        middle(v - 1)
                        middle(v)
                    v += 1

            with act.Fori(0, NG // 2) as it:
                for u in range(2):
                    g = 2 * it + u

                    def read_out(c, g=g):
                        act.wait_ge(pv_done, P_SLOTS + g * SS + (C_END[c] + 1))
                        act.wait_ge(o_stored[c % 2], 16 + (2 * g + c // 2) * (16 * 2 * HG))
                        nc.scalar.activation(O_sb[:, c % 2, :], OB[:, :], ACT.Copy).then_inc(o_out, 1)

                    for s in range(SS):
                        w = CW - step_off(s)
                        for p in range(2):
                            act.wait_ge(st_ready, g * (2 * SS) + (2 * s + p + 1))
                            if p == 0:
                                act.wait_ge(pv_done, g * SS + (s + 1))
                            nc.scalar.activation(probs[:, s % P_SLOTS, 2 * p:2 * p + 2, 0:w], ST[p][:, :, 0:w], ACT.Exp)\
                              .then_inc(exp_done, 1)
                        for c in range(NC - 1):
                            if s == C_END[c] + PV_LAG:
                                read_out(c)
                    read_out(NC - 1)

            for c in range(NC):
                for f in range(FC):
                    act.wait_ge(xt2_psum, 2 * c + f + 1)
                    if c >= 2 and f == 0:
                        act.wait_ge(ex_ready, (c - 1) * TC * (E // 2))
                    nc.scalar.activation(xT2[:, c % 2, f, :], MB[f][:, :], ACT.Copy).then_inc(xt2_ready, 1)
                act.wait_ge(gd_ready, c + 1)
                nc.scalar.activation(ge[:, :], gd[:, :], ACT.Exp).then_inc(ge_ready, 1)
                act.wait_ge(gt_psum, c + 1)
                if c >= 1:
                    act.wait_ge(gb_ready, 2 * c)
                nc.scalar.activation(gT[:, :], MB[1][0:E, :], ACT.Copy).then_inc(gt_ready, 1)

        @block.vector
        def _(dve):
            steps = [0]

            def link(ins):
                steps[0] += 1
                ins.then_inc(ln_step, 1)
                dve.wait_ge(ln_step, steps[0])

            norms = [0]

            def normalise(tile, put, done):
                for t in range(TC):
                    last = nc.vector.bn_stats(st6[:, t, :], tile(t))
                    if t < TC - 1:
                        steps[0] += 1
                        last.then_inc(ln_step, 1)
                link(last)
                for t in range(TC):
                    last = nc.vector.bn_aggr(mv[:, t, :], st6[:, t, :])
                    if t < TC - 1:
                        steps[0] += 1
                        last.then_inc(ln_step, 1)
                link(last)
                nc.vector.tensor_scalar(ve[:, :], mv[:, :, 1], EPS, None, ALU.add).then_inc(var_ready, 1)
                norms[0] += 1
                dve.wait_ge(rsqrt_ready, norms[0])
                link(nc.vector.scalar_tensor_tensor(ta[:, :], rs[:, :], -0.5, rs[:, :], ALU.mult, ALU.mult))
                link(nc.vector.tensor_tensor(tb[:, :], ta[:, :], ve[:, :], ALU.mult))
                link(nc.vector.scalar_tensor_tensor(ta[:, :], tb[:, :], 1.5, rs[:, :], ALU.add, ALU.mult))
                for t in range(TC):
                    last = nc.vector.tensor_scalar(put(t), tile(t), mv[:, t, 0:1], ta[:, t:t + 1],
                                                   ALU.subtract, ALU.mult)
                    if t < TC - 1:
                        steps[0] += 1
                        last.then_inc(ln_step, 1)
                last.then_inc(done, 1)

            def stream_entry(i, n, mrow_seen):
                m = STREAM[i]
                bank = MB[i % M_RING]
                dve.wait_ge(m_ready, n + 1)
                if m[0] == "turn":
                    slot = (m[1] + 1) % 2
                    if mrow_seen is not None:
                        dve.wait_ge(mrow[slot], mrow_seen)
                    nc.vector.tensor_copy(mT[:, slot, :], bank[0:3 * HG * TC, 0:P // 2].bitcast(BF16))\
                      .then_inc(m_done, 1)
                    return
                _, c, t, j, kc = m
                w = m_width(m)
                if kc < c:
                    nc.vector.tensor_reduce(pm[:, c, TC * j + t, kc:kc + 1], bank[:, 0:w], AX.X, ALU.max)\
                      .then_inc(m_done, 1)
                else:
                    if not (isinstance(n, int) and n < M_RING):
                        dve.wait_ge(m_done, n + 1 - m_free(i))
                    dve.sem_inc(dve_passed, 1)
                    nc.vector.tensor_tensor_reduce(
                        out=junk[:, i % M_RING, 0:w], in0=bank[:, 0:w], in1=tri[:, CW - w:CW], scale=1.0, scalar=NEG,
                        op0=ALU.add, op1=ALU.max, accum_out=pm[:, c, TC * j + t, kc:kc + 1]).then_inc(m_done, 1)

            def fold(c, n):
                dve.wait_ge(m_done, n + 1)
                nc.vector.tensor_reduce(mr[:, :], pm[:, c, :, :], AX.X, ALU.max, negate=True).then_inc(folded, 1)

            dve.wait_ge(w_loaded, 80)
            nc.vector.tensor_copy(id_b[:, :], id_f[:, :]).then_inc(consts_ready, 1)
            nc.vector.tensor_scalar(bqk_half[:, :, :], bqk[:, :, :], 0.5, None, ALU.mult).then_inc(bias_ready, 1)
            nc.vector.memset(mparts[:, :, :, :], 0.0).then_inc(consts_ready, 1)
            link(nc.vector.memset(pm[:, :, :, :], NEG))
            for c in range(NC):
                dve.wait_ge(x_loaded[c], 16)
                if c >= 2:
                    dve.wait_ge(pro_ready, 1 + PRO.index(("T", c - 2, 1)))
                normalise(lambda t: x_sb[:, TC * c + t, :], lambda t: xh[:, c % 2, t, :], xh_ready)
            dve.wait_ge(v_loaded, 64)
            for i in range(LEAD):
                stream_entry(i, i, None)
                if i in M_END:
                    fold(M_END.index(i), i)

            with dve.Fori(0, NG // 2) as it:
                for u in range(2):
                    g = 2 * it + u
                    m_base = LEAD + SN * g
                    for s in range(SS):
                        for i, following in BODY[s]:
                            seen = None
                            if STREAM[i][0] == "turn":
                                c = STREAM[i][1]
                                uses = {2: 1, 3: 1, 0: 2, 1: 2}[c]
                                seen = 48 * (2 * g + uses)
                            stream_entry(i, m_base + stream_place(i, following), seen)
                            if i in M_END:
                                fold(M_END.index(i), m_base + stream_place(i, following))

            dve.wait_ge(den_loaded, 16)
            nc.vector.reciprocal(rden_c[:, :], den_c[:, :]).then_inc(rden_ready, 1)

            def attn(c):
                dve.wait_ge(at_loaded[c % 2], 16 * 2 * FC * (c // 2 + 1))
                if c >= 1:
                    dve.wait_ge(wo_ready, 2 * c)
                nc.vector.tensor_tensor(at[:, :, :], nm[:, c % 2, :, :], rd[:, c % 2, :, :], ALU.mult)\
                  .then_inc(at_ready, 1)

            def residual(c):
                for h in range(2):
                    dve.wait_ge(wo_ready, 2 * c + h + 1)
                    rows = x_sb[:, TC * c + 2 * h:TC * c + 2 * h + 2, :].rearrange("p t d -> p (t d)")
                    nc.vector.tensor_tensor(rows, PB[h][:, :], rows, ALU.add).then_inc(x1_ready, 1)
                dve.wait_ge(x1_ready, 2 * (c + 1))
                if c >= 1:
                    dve.wait_ge(xt2_psum, 2 * c)
                normalise(lambda t: x_sb[:, TC * c + t, :], lambda t: xh2[:, t, :], xh2_ready)

            def route(c):
                dve.wait_ge(lg_ready, c + 1)
                nc.vector.tensor_copy(lg[:, :, :], MB[0][:, 0:TC * E].rearrange("p (t e) -> p t e", e=E))\
                  .then_inc(lg_read, 1)
                dve.wait_ge(lg_read, c + 1)
                for t in range(TC):
                    link(nc.vector.max(top[:, t, :], lg[:, t, :]))
                for t in range(TC):
                    link(nc.vector.max_index(idx[:, t, :], top[:, t, :], lg[:, t, :]))
                nc.vector.tensor_tensor(gd[:, :], top[:, :, 1], top[:, :, 0], ALU.subtract).then_inc(gd_ready, 1)
                link(nc.vector.tensor_copy(idf[:, :, :], idx[:, :, 0:2]))
                dve.wait_ge(ge_ready, c + 1)
                link(nc.vector.tensor_scalar(gs[:, :], ge[:, :], 1.0, None, ALU.add))
                link(nc.vector.reciprocal(gw[:, :, 0], gs[:, :]))
                link(nc.vector.tensor_tensor(gw[:, :, 1], gw[:, :, 0], ge[:, :], ALU.mult))
                for t in range(TC):
                    for n, dst in ((0, g1), (1, g2)):
                        steps[0] += 1
                        nc.vector.tensor_scalar(dst[:, t, :], iota[:, :], idf[:, t, n:n + 1], gw[:, t, n:n + 1],
                                                ALU.is_equal, ALU.mult).then_inc(ln_step, 1)
                dve.wait_ge(ln_step, steps[0])
                nc.vector.tensor_tensor(gates[:, c % 2, :, :], g1[:, :, :], g2[:, :, :], ALU.add)\
                  .then_inc(gates_ready, 1)
                dve.wait_ge(gates_ready, c + 1)

            def begin(c):
                if c >= 2:
                    dve.wait_ge(y_stored[c % 2], 16 * TC * (c // 2))
                for h in range(2):
                    dve.wait_ge(gb_ready, 2 * c + h + 1)
                    rows = slice(2 * h, 2 * h + 2)
                    nc.vector.tensor_tensor(
                        yb[:, c % 2, rows, :].rearrange("p t d -> p (t d)"), PB[h][:, :],
                        x_sb[:, TC * c + 2 * h:TC * c + 2 * h + 2, :].rearrange("p t d -> p (t d)"), ALU.add)\
                        .then_inc(yb_ready, 1)
                dve.wait_ge(yb_ready, 2 * (c + 1))

            def combine(c, t):
                y = yb[:, c % 2, t, :]
                for e2 in range(E // 2):
                    n = (TC * c + t) * (E // 2) + e2
                    dve.wait_ge(ex_ready, n + 1)
                    for h in range(2):
                        e = 2 * e2 + h
                        ins = nc.vector.scalar_tensor_tensor(
                            out=y, in0=ring4[n % 4][:, F * h:F * (h + 1)], scalar=gates[:, c % 2, t, e:e + 1],
                            in1=y, op0=ALU.mult, op1=ALU.add)
                        if h == 0:
                            link(ins)
                        else:
                            ins.then_inc(ex_done, 1)
                            dve.wait_ge(ex_done, n + 1)

            attn(0)
            dve.wait_ge(xb_ready, NC)
            residual(0)
            route(0)
            for c in range(NC):
                more = c + 1 < NC
                if more:
                    attn(c + 1)
                begin(c)
                combine(c, 0)
                combine(c, 1)
                if more:
                    residual(c + 1)
                combine(c, 2)
                combine(c, 3)
                if more:
                    route(c + 1)

        @block.gpsimd
        def _(pool):
            steps = [0]

            def link(ins):
                steps[0] += 1
                ins.then_inc(vg_set, 1)
                pool.wait_ge(vg_set, steps[0])

            def split_maxima(c, number):
                split = mparts[:, (c + 1) % 2, :, :]
                pool.wait_ge(folded, number)

                pool.sem_inc(pool_passed, 1)

                def step(k, ins):
                    ins.then_inc(mpost_step, 1)
                    pool.wait_ge(mpost_step, (number - 1) * 3 + k)
                    pool.sem_inc(pool_passed, 1)

                step(1, nc.gpsimd.tensor_copy(split[:, 0, :], mr[:, :]))
                step(2, nc.gpsimd.tensor_tensor(mx[:, :], mr[:, :], split[:, 0, :], ALU.subtract))
                step(3, nc.gpsimd.tensor_copy(split[:, 1, :], mx[:, :]))
                nc.gpsimd.tensor_tensor(split[:, 2, :], mx[:, :], split[:, 1, :], ALU.subtract)\
                    .then_inc(mparts_ready, 1)

            def split_pair(v):
                for k in (v, v + 1):
                    pool.wait_ge(high_ready, k + 1)
                    nc.gpsimd.tensor_tensor(r1[:, k % 2, :], qf[:, k % 2, :], parts[:, k % 2, 0, :], ALU.subtract)\
                        .then_inc(rest_ready, 1)
                for k in (v, v + 1):
                    pool.wait_ge(mid_ready, k + 1)
                    nc.gpsimd.tensor_tensor(parts[:, k % 2, 2, :], r1[:, k % 2, :], parts[:, k % 2, 1, :],
                                            ALU.subtract).then_inc(low_ready, 1)

            def bias_values(k):
                pool.wait_ge(pro_done, PRO_F1 + 2 * (k + 1))
                rows = V[:, TC * k:TC * (k + 1), :]
                nc.gpsimd.tensor_tensor(rows, rows, bv_sb[:, :].unsqueeze(1).broadcast_to([P, TC, D]), ALU.add)\
                    .then_inc(v_biased, 1)

            def copy_values(b, col):
                src = V[:, :, bass.ds(col, HG * DH)].rearrange("p k (j d) -> p k j d", d=DH)
                pool.sem_inc(pool_passed, 1)
                nc.gpsimd.tensor_copy(Vg[b][:, :, :, 0:DH], src).then_inc(vg_ready, 1)

            nc.gpsimd.memset(Ko[0][SR:SX, :, :], 1.0).then_inc(ones_ready, 1)
            pool.wait_ge(ones_ready, 1)
            for e in range(E):
                steps[0] += 1
                nc.gpsimd.memset(iota[:, e:e + 1], float(e)).then_inc(vg_set, 1)
            for b in range(2):
                link(nc.gpsimd.memset(Vg[b][:, :, :, DH:VW], 0.0))
                link(nc.gpsimd.memset(Vg[b][:, :, :, DH:DH + 1], 1.0))
            link(nc.gpsimd.memset(neg_half[:, :], -0.5))
            norms = [0]

            def rsqrt():
                norms[0] += 1
                pool.wait_ge(var_ready, norms[0])
                nc.gpsimd.tensor_tensor(rs[:, :], ve[:, :], neg_half[:, :], ALU.pow).then_inc(rsqrt_ready, 1)

            rsqrt()
            rsqrt()
            for c in range(NC):
                split_pair(2 * c)
                if c + 2 < NC:
                    rsqrt()
            pool.wait_ge(v_loaded, 64)
            bias_values(0)
            bias_values(1)
            split_maxima(0, 1)
            bias_values(2)
            bias_values(3)
            pool.wait_ge(v_biased, NC)
            copy_values(0, 0)
            split_pair(2 * NC)
            split_maxima(1, 2)
            for c in range(1, NC):
                split_pair(2 * NC + 2 * c)
            for c in range(NC):
                rows = x_sb[:, TC * c:TC * (c + 1), :]
                pool.wait_ge(xh_ready, c + 1)
                nc.gpsimd.tensor_tensor(rows, rows, bo_sb[:, :].unsqueeze(1).broadcast_to([P, TC, D]), ALU.add)\
                    .then_inc(xb_ready, 1)

            with pool.Fori(0, NG // 2) as it:
                for u in range(2):
                    g = 2 * it + u
                    m_base = LEAD + SN * g
                    pool.wait_ge(pv_done, P_SLOTS + SS * g)
                    pool.sem_inc(pool_passed, 1)
                    copy_values(1 - u, (2 * it + 1) * (HG * DH) if u == 0 else (1 - it) * (2 * HG * DH))
                    for s in range(SS):
                        c, _ = STEPS[s]
                        if diag(s) is not None:
                            pool.wait_ge(exp_done, g * (2 * SS) + (2 * s + 4))
                            pool.sem_inc(pool_passed, 1)
                            block_ = probs[:, s % P_SLOTS, :, 0:P]
                            nc.gpsimd.affine_select(out=block_, in_=block_, compare_op=ALU.is_ge, fill=0.0, base=0,
                                                    pattern=[[0, HG], [1, P]], channel_multiplier=-1)\
                                .then_inc(mask_done, 1)
                        for i, following in BODY[s]:
                            if i in M_END:
                                place = stream_place(i, following)
                                split_maxima(M_END.index(i), NC * g + turn_number(place))

            for c in range(NC):
                rsqrt()


def kernel(L0_attn_X, L0_attn_Wq, L0_attn_bq, L0_attn_Wk, L0_attn_bk, L0_attn_Wv, L0_attn_bv, L0_attn_Wo, L0_attn_bo,
           L0_ffn_Wr, L0_ffn_We, L0_ffn_be):
    import numpy as np
    import concourse.bacc as bacc
    from concourse.bass_utils import run_bass_kernel_spmd

    def lay(a):
        return np.ascontiguousarray(a)

    arrays = {
        "X": lay(np.asarray(L0_attn_X).reshape(S, D)),
        "WqT": lay(np.asarray(L0_attn_Wq).T), "WkT": lay(np.asarray(L0_attn_Wk).T),
        "WvT": lay(np.asarray(L0_attn_Wv).T), "WoT": lay(np.asarray(L0_attn_Wo).T),
        "bq": lay(L0_attn_bq), "bk": lay(L0_attn_bk), "bv": lay(L0_attn_bv), "bo": lay(L0_attn_bo),
        "Wr": lay(L0_ffn_Wr), "We": lay(L0_ffn_We), "be": lay(L0_ffn_be),
        "ident": np.eye(P, dtype=np.float32),
        "trimask": np.where(np.arange(CW)[None, :] - (CW - P) <= np.arange(P)[:, None], 0.0, NEG).astype(np.float32),
    }
    nc = bacc.Bacc("TRN2", target_bir_lowering=False, num_devices=1)
    args, feed = {}, {}
    for name, a in arrays.items():
        feed["in_" + name] = a
        args[name] = nc.dram_tensor("in_" + name, a.shape, mybir.dt.from_np(a.dtype), kind="ExternalInput").ap()
    shape, dtype = (S, D), np.dtype("float32")
    out = nc.dram_tensor("out_y", shape, mybir.dt.from_np(dtype), kind="ExternalOutput").ap()
    build_program(nc, out=out, **args)
    r = run_bass_kernel_spmd(nc, [feed], core_ids=[0])
    return r.results[0]["out_y"].reshape(1, S, D)
```

```python
from contextlib import ExitStack

import concourse.bass as bass
from concourse import mybir
from concourse.alu_op_type import AluOpType as ALU

F32 = mybir.dt.float32
BF16 = mybir.dt.bfloat16
U32 = mybir.dt.uint32
ACT = mybir.ActivationFunctionType
AX = mybir.AxisListType

P = 128
S = 2048
D = 256
H = 16
DH = D // H
E = 8
F = 256
EPS = 1e-5
NEG = -1e30

FC = D // P
NT = S // P
CW = 512
NC = S // CW
TC = CW // P
HG = 4
NG = H // HG
PARTS = 3
RUNS = [(0, 3, 0), (1, 2, 3), (2, 1, 5)]
TERMS = sum(copies for _, copies, _ in RUNS)
SR = TERMS * DH
SX = SR + 3
VW = 32

M_RING = 3
M_LAG = 12


def max_stream():
    out = []
    for c in range(NC):
        blocks = [("max", c, t, j, kc) for t in range(TC) for j in range(HG) for kc in range(c + 1)]
        out += blocks[:M_LAG] + [("turn", (c - 1) % NC)] + blocks[M_LAG:]
    return out


STREAM = max_stream()
SN = len(STREAM)
M_END = [max(i for i, m in enumerate(STREAM) if m[0] == "max" and m[1] == c) for c in range(NC)]
LEAD = 92


def m_free(i):
    return M_RING if i >= SN % M_RING else SN % M_RING


def m_width(m):
    if m[0] == "turn":
        return P
    _, c, t, _, kc = m
    return CW if kc < c else (t + 1) * P


STEPS = [(c, kt) for c in range(NC) for kt in range(TC * (c + 1))]
SS = len(STEPS)
C_END = [max(s for s, (c, _) in enumerate(STEPS) if c == cc) for cc in range(NC)]
PV_LAG = 2
P_SLOTS = 4
DIAGS = NC * TC


def diag(s):
    c, kt = STEPS[s]
    return kt - TC * c if kt >= TC * c else None


def step_off(s):
    return P * (diag(s) or 0)


def body_stream():
    order = [(i, False) for i in range(LEAD, SN)] + [(i, True) for i in range(LEAD)]
    m_total = sum(m_width(m) for m in STREAM)
    s_total = sum(CW - step_off(s) for s in range(SS))
    out, at, m_cols, s_cols = [], 0, 0, 0
    for s in range(SS):
        s_cols += CW - step_off(s)
        mine = []
        while at < SN and (m_cols < m_total * s_cols / s_total or s == SS - 1):
            mine.append(order[at])
            m_cols += m_width(STREAM[order[at][0]])
            at += 1
        out.append(mine)
    return out


BODY = body_stream()


def stream_place(i, following):
    return SN - LEAD + i if following else i - LEAD


TURNS_BEFORE = sum(m[0] == "turn" for m in STREAM[1 + M_LAG:LEAD])


def turn_number(place):
    return 1 + TURNS_BEFORE + sum(m[0] == "turn" for m in (STREAM[LEAD:] + STREAM[:LEAD])[:place])


def build_program(nc, X, WqT, WkT, WvT, WoT, bq, bk, bv, bo, Wr, We, be, ident, trimask, out):
    ctx = ExitStack()
    with ctx:
        def sb(name, shape, dt=F32):
            return ctx.enter_context(nc.sbuf_tensor(name, shape, dt))

        def sem(name):
            return ctx.enter_context(nc.semaphore(name))

        qk_d = nc.dram_tensor("qk_parts", [2, NG, NC, PARTS, DH, HG * CW], BF16, kind="Internal").ap()
        o_d = nc.dram_tensor("attn_sums", [NC, H, VW, CW], F32, kind="Internal").ap()
        rden_d = nc.dram_tensor("attn_rden", [NC, H, CW], F32, kind="Internal").ap()

        x_sb = sb("x_sb", [P, NT, D])
        wq, wk, wv, wo = (sb(n, [P, FC, D]) for n in ("wq", "wk", "wv", "wo"))
        we_sb = sb("we_sb", [P, FC, E * F])
        wr_sb = sb("wr_sb", [P, FC, E])
        be_sb = sb("be_sb", [E, F])
        bv_sb = sb("bv_sb", [P, D])
        bo_sb = sb("bo_sb", [P, D])
        bqk = sb("bqk", [P, 2, FC])
        bqk_half = sb("bqk_half", [P, 2, FC])
        id_f = sb("id_f", [P, P])
        id_b = sb("id_b", [P, P], BF16)
        tri = sb("tri", [P, CW])
        iota = sb("iota", [P, E])
        ones = sb("ones", [3, CW], BF16)
        parts = sb("parts", [P, 2, 3, CW], BF16)
        V = sb("V", [P, NT, D])
        Vg = [sb(f"Vg{b}", [P, NT, HG, VW]) for b in range(2)]
        Qo = [sb(f"Qo{b}", [P, NC, HG, CW], BF16) for b in range(2)]
        Ko = [sb(f"Ko{b}", [P, NC, HG, CW], BF16) for b in range(2)]
        probs = sb("probs", [P, P_SLOTS, HG, CW])
        O_sb = sb("O_sb", [P, 2, CW])
        junk = sb("junk", [P, M_RING, CW], BF16)
        pm = sb("pm", [P, NC, HG * TC, NC])
        mx = sb("mx", [P, HG * TC])
        mr = sb("mr", [P, HG * TC])
        mparts = sb("mparts", [P, 2, 5, HG * TC], BF16)
        mT = sb("mT", [3 * HG * TC, 2, P], BF16)
        st6 = sb("st6", [P, TC, 6])
        mv = sb("mv", [P, 2, TC, 2])
        ve = sb("ve", [P, 2, TC])
        rs = sb("rs", [P, 2, TC])
        ta = sb("ta", [P, TC])
        neg_half = sb("neg_half", [P, TC])
        tb = sb("tb", [P, TC])
        den_c = sb("den_c", [P, H * S // P])
        rden_c = sb("rden_c", [P, H * S // P])
        lg = sb("lg", [P, TC, E])
        top = sb("top", [P, TC, 8])
        idx = sb("idx", [P, TC, 8], U32)
        idf = sb("idf", [P, TC, 2])
        gd = sb("gd", [P, TC])
        ge = sb("ge", [P, TC])
        gs = sb("gs", [P, TC])
        gw = sb("gw", [P, TC, 2])
        g1 = sb("g1", [P, TC, E])
        g2 = sb("g2", [P, TC, E])
        gT = sb("gT", [E, CW])
        gates = sb("gates", [P, 2, TC, E])

        q1f = Qo[1][:, :, :, :].rearrange("p c j w -> p (c j w)").bitcast(F32)
        xT = Ko[1][:, :, :, :].rearrange("p c j w -> p (c j w)").bitcast(F32).rearrange("p (f s) -> p f s", f=FC)
        xh = q1f[:, 0:2 * TC * D].rearrange("p (b t d) -> p b t d", b=2, t=TC)
        qf = q1f[:, 2048:3072].rearrange("p (b w) -> p b w", b=2)
        r1 = q1f[:, 3072:4096].rearrange("p (b w) -> p b w", b=2)
        pr = probs[:, :, :, :].rearrange("p a j w -> p (a j w)")
        nm = pr[:, 0:2048].rearrange("p (b f w) -> p b f w", b=2, f=FC)
        rd = pr[:, 2048:4096].rearrange("p (b f w) -> p b f w", b=2, f=FC)
        at = pr[:, 4096:5120].rearrange("p (f w) -> p f w", f=FC)
        xh2 = pr[:, 5120:6144].rearrange("p (t d) -> p t d", t=TC)
        xT2 = pr[:, 6144:8192].rearrange("p (b f w) -> p b f w", b=2, f=FC)
        yb = V[:, 0:2 * TC, :].rearrange("p (b t) d -> p b t d", b=2)

        ST = [ctx.enter_context(nc.psum_tensor(f"ST{i}", [P, 2, CW], F32)) for i in range(2)]
        MB = [ctx.enter_context(nc.psum_tensor(f"MB{i}", [P, CW], F32)) for i in range(M_RING)]
        OB = ctx.enter_context(nc.psum_tensor("OB", [P, CW], F32))
        PB = [OB, MB[2]]
        ring4 = [ST[0][:, 0, :], ST[0][:, 1, :], ST[1][:, 0, :], ST[1][:, 1, :]]

        x_loaded = [sem(f"x_loaded{c}") for c in range(NC)]
        id_loaded, w_loaded, v_loaded, e_loaded = sem("id_loaded"), sem("w_loaded"), sem("v_loaded"), sem("e_loaded")
        tri_loaded, biases_loaded = sem("tri_loaded"), sem("biases_loaded")
        consts_ready = sem("consts_ready")
        var_ready, rsqrt_ready = sem("var_ready"), sem("rsqrt_ready")
        ln_step = sem("ln_step")
        xh_ready = sem("xh_ready")
        pro_ready, pro_done = sem("pro_ready"), sem("pro_done")
        bias_ready = sem("bias_ready")
        qf_ready, high_ready, rest_ready, mid_ready, low_ready = (
            sem(n) for n in ("qf_ready", "high_ready", "rest_ready", "mid_ready", "low_ready"))
        parts_stored = [[sem(f"parts_stored{i}{half}") for half in range(2)] for i in range(2)]
        vg_set, vg_ready = sem("vg_set"), sem("vg_ready")
        ones_ready, ones_placed = sem("ones_ready"), [sem(f"ones_placed{b}") for b in range(2)]
        xb_ready, iota_ready = sem("xb_ready"), sem("iota_ready")
        first_ops = [sem(f"first_ops{c}") for c in range(NC)]
        ops_loaded = [sem(f"ops_loaded{b}") for b in range(2)]
        m_ready, m_done = sem("m_ready"), sem("m_done")
        folded = sem("folded")
        mpost_step = sem("mpost_step")
        mparts_ready = sem("mparts_ready")
        mrow = [sem(f"mrow{i}") for i in range(2)]
        st_ready, exp_done = sem("st_ready"), sem("exp_done")
        mask_done, pv_done = sem("mask_done"), sem("pv_done")
        o_out = sem("o_out")
        o_stored = [sem(f"o_stored{i}") for i in range(2)]
        den_loaded, rden_ready, rden_stored = sem("den_loaded"), sem("rden_ready"), sem("rden_stored")
        at_loaded = [sem(f"at_loaded{i}") for i in range(2)]
        at_ready, wo_ready, x1_ready = sem("at_ready"), sem("wo_ready"), sem("x1_ready")
        xh2_ready, xt2_psum, xt2_ready = sem("xh2_ready"), sem("xt2_psum"), sem("xt2_ready")
        lg_ready, gd_ready, ge_ready, gates_ready = sem("lg_ready"), sem("gd_ready"), sem("ge_ready"), sem("gates_ready")
        lg_read = sem("lg_read")
        ex_ready, ex_done = sem("ex_ready"), sem("ex_done")
        gt_psum, gt_ready, gb_ready, yb_ready = sem("gt_psum"), sem("gt_ready"), sem("gb_ready"), sem("yb_ready")
        y_stored = [sem(f"y_stored{i}") for i in range(2)]
        dve_passed, pool_passed, sp_passed = sem("dve_passed"), sem("pool_passed"), sem("sp_passed")

        BANK_PARTS = {"T": 1, "QK": 2, "V": 2}
        M_AFTER = 6

        def prologue_plan():
            def qk(c, f):
                return [("QK", c, f, side) for side in range(2)]

            def t(c):
                return [("T", c, f) for f in range(FC)]

            def parts_of(banks):
                return [(item, k) for item in banks for k in range(BANK_PARTS[item[0]])]

            head = parts_of(t(0) + qk(0, 0) + [("V", 0)] + t(1) + qk(1, 0) + [("V", 1)] + t(2) + [("V", 2)])
            rest = parts_of(qk(2, 0) + t(3) + qk(3, 0) + [("V", 3)] + qk(0, 1) + [("V", 4), ("V", 5)] + qk(1, 1)
                            + [("V", 6), ("V", 7)] + qk(2, 1) + qk(3, 1))
            plan, at = list(head), 0
            for n in range(LEAD):
                while at < len(rest) and at * (LEAD - M_AFTER) <= n * len(rest):
                    plan.append(rest[at])
                    at += 1
                plan.append((("M", n), 0))
            return plan

        PLAN = prologue_plan()
        DONE = [item for item, part in PLAN if part == BANK_PARTS.get(item[0], 1) - 1]
        PRO = [item for item in DONE if item[0] != "M"]
        M_CHUNK_START = [0] + [e + 1 for e in M_END[:-1]]

        block = ctx.enter_context(nc.Block())

        @block.sync
        def _(sp):
            xv = X.rearrange("(c t p) d -> c p t d", t=TC, p=P)

            def load_x(c):
                sp.dma_start(x_sb[:, TC * c:TC * (c + 1), :], xv[c]).then_inc(x_loaded[c], 16)

            for i in range(2):
                sp.sem_inc(o_stored[i], 16)
            load_x(0)
            sp.dma_start(id_f[:, :], ident).then_inc(id_loaded, 16)
            sp.dma_start(wq[:, :, :], WqT.rearrange("(a p) n -> p a n", p=P)).then_inc(w_loaded, 16)
            sp.dma_start(wk[:, :, :], WkT.rearrange("(a p) n -> p a n", p=P)).then_inc(w_loaded, 16)
            load_x(1)
            for side, b in enumerate((bq, bk)):
                sp.dma_start(bqk[:, side, :], b.rearrange("(a p) -> p a", p=P),
                             allow_slow_non_contiguous=True).then_inc(w_loaded, 16)
            sp.dma_start(wv[:, :, :], WvT.rearrange("(a p) n -> p a n", p=P)).then_inc(v_loaded, 16)
            for c in range(2, NC):
                load_x(c)
            sp.dma_start(tri[:, :], trimask).then_inc(tri_loaded, 16)
            sp.dma_start(bv_sb[:, :], bv.partition_broadcast(P)).then_inc(biases_loaded, 16)
            sp.dma_start(bo_sb[:, :], bo.partition_broadcast(P)).then_inc(biases_loaded, 16)

            def store_parts(v, c, f, side):
                sp.wait_ge(low_ready, v + 1)
                for half in range(2):
                    dst = qk_d[side, 2 * f + half, c].rearrange("a d (j q) -> (d j) a q", q=CW)
                    sp.dma_start(dst, parts[P // 2 * half:P // 2 * (half + 1), v % 2, :, :])\
                      .then_inc(parts_stored[v % 2][half], 16)

            def load_first(c):
                for slot in range(2):
                    sp.wait_ge(parts_stored[slot][0], 16 * (c + 1))
                for part, copies, block_ in RUNS:
                    rows = slice(DH * block_, DH * (block_ + copies))
                    sp.dma_start(Qo[0][rows, c, :, :], qk_d[0, 0, c, part].unsqueeze(0)
                                 .broadcast_to([copies, DH, HG * CW])).then_inc(first_ops[c], 16)
                    sp.dma_start(Ko[0][rows, c, :, :], qk_d[1, 0, c, 0:copies]).then_inc(first_ops[c], 16)

            def load_group(b, group):
                for part, copies, block_ in RUNS:
                    rows = slice(DH * block_, DH * (block_ + copies))
                    for copy in range(copies):
                        at_ = DH * (block_ + copy)
                        sp.dma_start(Qo[b][at_:at_ + DH, :, :, :],
                                     qk_d[0, bass.ds(group, 1), :, part].rearrange("g c d q -> d (g c) q"))\
                          .then_inc(ops_loaded[b], 16)
                    sp.dma_start(Ko[b][rows, :, :, :], qk_d[1, bass.ds(group, 1), :, 0:copies]
                                 .rearrange("g c a d q -> (a d) (g c) q")).then_inc(ops_loaded[b], 16)

            def place_row(b, c, slot, m_seen):
                sp.wait_ge(m_done, m_seen)
                for n in range(3):
                    sp.dma_start(Qo[b][SR + n:SR + n + 1, c, :, :], mT[HG * TC * n:HG * TC * (n + 1), slot, :])\
                      .then_inc(mrow[slot], 16)

            def place_ones(b):
                sp.wait_ge(ones_ready, 1)
                sp.dma_start(Ko[b][SR:SX, :, :, :].rearrange("p c j w -> p (c j) w"),
                             ones[:, :].unsqueeze(1).broadcast_to([3, HG * NC, CW])).then_inc(ones_placed[b], 16)

            v = 0
            place_ones(0)
            for item in DONE:
                if item[0] == "QK":
                    _, c, f, side = item
                    store_parts(v, c, f, side)
                    if f == 0 and side == 1:
                        load_first(c)
                    v += 1
                elif item[0] == "M" and STREAM[item[1]][0] == "turn" and item[1] > M_LAG:
                    c = STREAM[item[1]][1]
                    place_row(0, c, (c + 1) % 2, item[1] + 1)
            sp.dma_start(wo[:, :, :], WoT.rearrange("(a p) n -> p a n", p=P)).then_inc(e_loaded, 16)
            sp.dma_start(wr_sb[:, :, :], Wr.rearrange("(a p) e -> p a e", p=P)).then_inc(e_loaded, 16)
            for e in range(E):
                sp.dma_start(we_sb[:, :, F * e:F * (e + 1)], We[e].rearrange("(a p) f -> p a f", p=P))\
                  .then_inc(e_loaded, 16)
            sp.dma_start(be_sb[:, :], be).then_inc(e_loaded, 16)
            for slot in range(2):
                for half in range(2):
                    sp.wait_ge(parts_stored[slot][half], 16 * 2 * NC)

            sp.wait_ge(st_ready, 1)
            place_ones(1)

            with sp.Fori(0, NG // 2) as it:
                for u in range(2):
                    m_base = LEAD + SN * (2 * it + u)
                    sp.wait_ge(st_ready, (2 * it + u) * (2 * SS) + 1)
                    sp.sem_inc(sp_passed, 1)
                    load_group(1 - u, 2 * it + 1 if u == 0 else (1 - it) * 2)
                    for s in range(SS):
                        for i, following in BODY[s]:
                            if STREAM[i][0] == "turn":
                                c = STREAM[i][1]
                                b = 1 - u if following and i > M_LAG else u
                                place_row(b, c, (c + 1) % 2, m_base + (stream_place(i, following) + 1))
                        for c in range(NC):
                            if s == min(C_END[c] + PV_LAG + 1, SS - 1):
                                sp.wait_ge(o_out, (2 * it + u) * NC + (c + 2))
                                sp.dma_start(o_d[c, bass.ds(it * (2 * HG) + u * HG, HG), :, :]
                                             .rearrange("h d q -> (h d) q"), O_sb[:, c % 2, :])\
                                  .then_inc(o_stored[c % 2], 16)

            for i in range(2):
                sp.wait_ge(o_stored[i], 16 + 16 * (NG * NC // 2))
            for c in range(NC):
                sp.dma_start(den_c[:, CW * H // P * c:CW * H // P * (c + 1)],
                             o_d[c, :, DH, :].rearrange("h (a w) -> h a w", w=CW * H // P)).then_inc(den_loaded, 16)

            hs = P // DH

            def load_num(c):
                for f in range(FC):
                    sp.dma_start(nm[:, c % 2, f, :], o_d[c, hs * f:hs * (f + 1), 0:DH, :])\
                      .then_inc(at_loaded[c % 2], 16)

            def load_rden(c):
                for f in range(FC):
                    src = rden_d[c, hs * f:hs * (f + 1), :]
                    sp.dma_start(rd[:, c % 2, f, :], src.unsqueeze(1).broadcast_to([hs, DH, CW]))\
                      .then_inc(at_loaded[c % 2], 16)

            sp.wait_ge(pv_done, P_SLOTS + NG * SS)
            load_num(0)
            load_num(1)
            sp.wait_ge(rden_ready, 1)
            for c in range(NC):
                sp.dma_start(rden_d[c].rearrange("h (a w) -> (h a) w", w=CW * H // P),
                             rden_c[:, CW * H // P * c:CW * H // P * (c + 1)]).then_inc(rden_stored, 16)
            sp.wait_ge(rden_stored, 16 * NC)
            load_rden(0)
            load_rden(1)
            ov = out.rearrange("(n p) d -> n p d", p=P)
            for c in range(NC):
                if c + 2 < NC:
                    sp.wait_ge(at_ready, c + 1)
                    load_num(c + 2)
                    load_rden(c + 2)
                for t in range(TC):
                    sp.wait_ge(ex_done, (TC * c + t + 1) * (E // 2))
                    sp.dma_start(ov[TC * c + t], yb[:, c % 2, t, :]).then_inc(y_stored[c % 2], 16)
            for i in range(2):
                sp.wait_ge(y_stored[i], 16 * NT // 2)

        @block.tensor
        def _(pe):
            def stream_entry(i, b, n, turn):
                m = STREAM[i]
                if not (isinstance(n, int) and n < M_RING):
                    pe.wait_ge(m_done, n + 1 - m_free(i))
                bank = MB[i % M_RING]
                if m[0] == "turn":
                    if not (isinstance(turn, int) and turn == 0):
                        pe.wait_ge(mparts_ready, turn)
                    slot = (m[1] + 1) % 2
                    nc.tensor.transpose(bank[0:5 * HG * TC, 0:P // 2].bitcast(BF16),
                                        mparts[:, slot, :, :].rearrange("p a m -> p (a m)"), id_b[:, :])\
                      .then_inc(m_ready, 1)
                    return
                _, c, t, j, kc = m
                w = m_width(m)
                nc.tensor.matmul(bank[:, 0:w], Qo[b][0:SR, c, j, P * t:P * (t + 1)],
                                 Ko[b][0:SR, kc, j, 0:w], start=True, stop=True).then_inc(m_ready, 1)

            def pro_bank(n, item, part):
                if n >= 4 and part == 0:
                    pe.wait_ge(pro_done, n - 3)
                bank = ring4[n % 4]
                if item[0] == "T":
                    _, c, f = item
                    if f == 0:
                        pe.wait_ge(xh_ready, c + 1)
                    for t in range(TC):
                        last = nc.tensor.transpose(bank[:, P * t:P * (t + 1)], xh[:, c % 2, t, P * f:P * (f + 1)],
                                                   id_f[:, :])
                elif item[0] == "QK":
                    _, c, f, side = item
                    if part == 0:
                        pe.wait_ge(pro_done, 1 + PRO.index(("T", c, 1)))
                    last = nc.tensor.matmul(bank, (wq, wk)[side][:, part, P * f:P * (f + 1)],
                                            xT[:, part, CW * c:CW * (c + 1)], start=(part == 0), stop=(part == 1))
                else:
                    if n == PRO.index(("V", 0)) and part == 0:
                        pe.wait_ge(v_loaded, 16)
                    if part == 0:
                        pe.wait_ge(pro_done, 1 + PRO.index(("T", 2 * item[1] // TC, 1)))
                    kt = 2 * item[1] + part
                    for a in range(FC):
                        last = nc.tensor.matmul(bank[:, D * part:D * (part + 1)], xT[:, a, P * kt:P * (kt + 1)],
                                                wv[:, a, :], start=(a == 0), stop=(a == FC - 1))
                if part == BANK_PARTS[item[0]] - 1:
                    last.then_inc(pro_ready, 1)

            pe.sem_inc(pv_done, P_SLOTS)
            pe.wait_ge(id_loaded, 16)
            n = turns = 0
            for item, part in PLAN:
                if item[0] != "M":
                    if item == ("QK", 0, 0, 0) and part == 0:
                        pe.wait_ge(w_loaded, 64)
                    pro_bank(n, item, part)
                    n += part == BANK_PARTS[item[0]] - 1
                    continue
                i = item[1]
                if i == 0:
                    pe.wait_ge(consts_ready, 2)
                if i in M_CHUNK_START:
                    pe.wait_ge(first_ops[M_CHUNK_START.index(i)], 16 * 2 * len(RUNS))
                stream_entry(i, 0, i, turns)
                turns += STREAM[i][0] == "turn"

            for c in range(NC):
                if M_CHUNK_START[c] >= LEAD:
                    pe.wait_ge(first_ops[c], 16 * 2 * len(RUNS))
            pe.wait_ge(pro_done, len(PRO))

            with pe.Fori(0, NG // 2) as it:
                for u in range(2):
                    g = 2 * it + u
                    m_base = LEAD + SN * g

                    def scores(s, j, u=u, g=g, it=it):
                        c, kt = STEPS[s]
                        w = CW - step_off(s)
                        if kt == 0 and j == 0:
                            slot = (c + 1) % 2
                            pe.wait_ge(mrow[slot], 48 * (2 * g + (c // 2 + 1)))
                        p = j // 2
                        if j % 2 == 0:
                            pe.wait_ge(exp_done, g * (2 * SS) + (2 * s + p + 1))
                        ins = nc.tensor.matmul(ST[p][:, j % 2, 0:w], Ko[u][0:SX, kt // TC, j, P * (kt % TC):P * (kt % TC + 1)],
                                               Qo[u][0:SX, c, j, CW - w:CW], start=True, stop=True)
                        if j % 2:
                            ins.then_inc(st_ready, 1)

                    def values(s, u=u, g=g, it=it):
                        c, kt = STEPS[s]
                        w = CW - step_off(s)
                        if kt == 0:
                            pe.wait_ge(o_out, g * NC + (c + 1))
                        if diag(s) is None:
                            pe.wait_ge(exp_done, g * (2 * SS) + (2 * s + 2 + 2))
                        else:
                            pe.wait_ge(mask_done, g * DIAGS + (TC * c + diag(s) + 1))
                        for j in range(HG):
                            last = nc.tensor.matmul(
                                OB[32 * j:32 * j + VW, CW - w:CW], Vg[u][:, kt, j, :],
                                probs[:, s % P_SLOTS, j, 0:w], start=(kt == 0), stop=(kt == TC * (c + 1) - 1),
                                tile_position=(0, 32 * j))
                        last.then_inc(pv_done, 1)

                    pe.wait_ge(vg_ready, g + 1)
                    pe.wait_ge(ones_placed[u], 16)
                    for s in range(SS):
                        between = [[] for _ in range(HG + 1)]
                        for k, entry in enumerate(BODY[s]):
                            between[(2 * k + 1) * (HG + 1) // (2 * len(BODY[s]))].append(entry)
                        for j in range(HG + 1):
                            if j < HG:
                                scores(s, j)
                            elif s >= PV_LAG:
                                values(s - PV_LAG)
                            for i, following in between[j]:
                                if following and i == 0:
                                    pe.wait_ge(ops_loaded[1 - u], (it + 1) * (16 * (TERMS + len(RUNS))))
                                place = stream_place(i, following)
                                stream_entry(i, 1 - u if following else u, m_base + place,
                                             NC * g + turn_number(place))
                    for s in range(SS - PV_LAG, SS):
                        values(s)

            pe.wait_ge(e_loaded, 16 * (3 + E))

            def project(c):
                pe.wait_ge(at_ready, c + 1)
                for h in range(2):
                    if c == 0:
                        if h == 0:
                            pe.wait_ge(o_out, NG * NC + 1)
                        else:
                            pe.wait_ge(m_done, LEAD + SN * NG)
                    else:
                        pe.wait_ge(yb_ready, 2 * (c - 1) + h + 1)
                    for t in range(2):
                        tok = P * (2 * h + t)
                        for a in range(FC):
                            last = nc.tensor.matmul(PB[h][:, D * t:D * (t + 1)], at[:, a, tok:tok + P], wo[:, a, :],
                                                    start=(a == 0), stop=(a == FC - 1))
                    last.then_inc(wo_ready, 1)

            def turn(c):
                pe.wait_ge(xh2_ready, c + 1)
                for f in range(FC):
                    if c == 0:
                        pe.wait_ge(m_done, LEAD + SN * NG)
                    elif f == 0:
                        pe.wait_ge(lg_read, c)
                        pe.wait_ge(xt2_ready, 2 * c)
                    for t in range(TC):
                        last = nc.tensor.transpose(MB[f][:, P * t:P * (t + 1)], xh2[:, t, P * f:P * (f + 1)], id_f[:, :])
                    last.then_inc(xt2_psum, 1)

            def logits(c):
                pe.wait_ge(xt2_ready, 2 * (c + 1))
                for t in range(TC):
                    for a in range(FC):
                        last = nc.tensor.matmul(MB[0][:, E * t:E * (t + 1)], xT2[:, c % 2, a, P * t:P * (t + 1)],
                                                wr_sb[:, a, :], start=(a == 0), stop=(a == FC - 1))
                last.then_inc(lg_ready, 1)

            def experts(c, t):
                for e2 in range(E // 2):
                    n = (TC * c + t) * (E // 2) + e2
                    if n >= 4:
                        pe.wait_ge(ex_done, n - 3)
                    elif n == 0:
                        pe.wait_ge(exp_done, 2 + NG * SS * 2)
                    for a in range(FC):
                        last = nc.tensor.matmul(ring4[n % 4], xT2[:, c % 2, a, P * t:P * (t + 1)],
                                                we_sb[:, a, 2 * F * e2:2 * F * (e2 + 1)],
                                                start=(a == 0), stop=(a == FC - 1))
                    last.then_inc(ex_ready, 1)

            def gated_bias(c):
                pe.wait_ge(gates_ready, c + 1)
                for t in range(TC):
                    last = nc.tensor.transpose(MB[1][0:E, P * t:P * (t + 1)], gates[:, c % 2, t, :], id_f[:, :])
                last.then_inc(gt_psum, 1)
                pe.wait_ge(gt_ready, c + 1)
                for h in range(2):
                    for t in range(2):
                        tok = P * (2 * h + t)
                        last = nc.tensor.matmul(PB[h][:, D * t:D * (t + 1)], gT[:, tok:tok + P], be_sb[:, :],
                                                start=True, stop=True)
                    last.then_inc(gb_ready, 1)

            project(0)
            turn(0)
            logits(0)
            for c in range(NC):
                more = c + 1 < NC
                experts(c, 0)
                gated_bias(c)
                experts(c, 1)
                if more:
                    project(c + 1)
                experts(c, 2)
                if more:
                    turn(c + 1)
                experts(c, 3)
                if more:
                    logits(c + 1)

        @block.scalar
        def _(act):
            act.sem_inc(exp_done, 2)
            act.sem_inc(o_out, 1)
            act.wait_ge(w_loaded, 64)
            nc.scalar.activation(bqk_half[:, :, :], bqk[:, :, :], ACT.Copy, scale=0.5).then_inc(bias_ready, 1)
            act.wait_ge(bias_ready, 1)
            v = 0
            pending = None

            def middle(v):
                act.wait_ge(rest_ready, v + 1)
                nc.scalar.activation(parts[:, v % 2, 1, :], r1[:, v % 2, :], ACT.Copy).then_inc(mid_ready, 1)

            for n, item in enumerate(PRO):
                act.wait_ge(pro_ready, n + 1)
                bank = ring4[n % 4]
                if item[0] == "T":
                    _, c, f = item
                    nc.scalar.activation(xT[:, f, CW * c:CW * (c + 1)], bank, ACT.Copy).then_inc(pro_done, 1)
                elif item[0] == "V":
                    kt = 2 * item[1]
                    nc.scalar.activation(V[:, kt:kt + 2, :].rearrange("p t d -> p (t d)"), bank, ACT.Copy)\
                      .then_inc(pro_done, 1)
                else:
                    _, c, f, side = item
                    if v >= 2:
                        act.wait_ge(rest_ready, v - 1)
                        for half in range(2):
                            act.wait_ge(parts_stored[v % 2][half], 16 * (v // 2))
                    nc.scalar.activation(qf[:, v % 2, :], bank, ACT.Identity, bias=bqk_half[:, side, f:f + 1],
                                         scale=0.5).then_inc(pro_done, 1)
                    act.wait_ge(pro_done, n + 1)
                    nc.scalar.activation(parts[:, v % 2, 0, :], qf[:, v % 2, :], ACT.Copy).then_inc(high_ready, 1)
                    if v % 2:
                        middle(v - 1)
                        middle(v)
                    v += 1

            with act.Fori(0, NG // 2) as it:
                for u in range(2):
                    g = 2 * it + u

                    def read_out(c, g=g):
                        act.wait_ge(pv_done, P_SLOTS + g * SS + (C_END[c] + 1))
                        act.wait_ge(o_stored[c % 2], 16 + (2 * g + c // 2) * 16)
                        nc.scalar.activation(O_sb[:, c % 2, :], OB[:, :], ACT.Copy).then_inc(o_out, 1)

                    for s in range(SS):
                        w = CW - step_off(s)
                        for p in range(2):
                            act.wait_ge(st_ready, g * (2 * SS) + (2 * s + p + 1))
                            if p == 0:
                                act.wait_ge(pv_done, g * SS + (s + 1))
                            nc.scalar.activation(probs[:, s % P_SLOTS, 2 * p:2 * p + 2, 0:w], ST[p][:, :, 0:w], ACT.Exp)\
                              .then_inc(exp_done, 1)
                        for c in range(NC - 1):
                            if s == C_END[c] + PV_LAG:
                                read_out(c)
                    read_out(NC - 1)

            for c in range(NC):
                for f in range(FC):
                    act.wait_ge(xt2_psum, 2 * c + f + 1)
                    if c >= 2 and f == 0:
                        act.wait_ge(ex_ready, (c - 1) * TC * (E // 2))
                    nc.scalar.activation(xT2[:, c % 2, f, :], MB[f][:, :], ACT.Copy).then_inc(xt2_ready, 1)
                act.wait_ge(gd_ready, c + 1)
                nc.scalar.activation(ge[:, :], gd[:, :], ACT.Exp).then_inc(ge_ready, 1)
                act.wait_ge(gt_psum, c + 1)
                if c >= 1:
                    act.wait_ge(gb_ready, 2 * c)
                nc.scalar.activation(gT[:, :], MB[1][0:E, :], ACT.Copy).then_inc(gt_ready, 1)

        @block.vector
        def _(dve):
            steps = [0]

            def link(ins):
                steps[0] += 1
                ins.then_inc(ln_step, 1)
                dve.wait_ge(ln_step, steps[0])

            def moments(n, tile):
                for t in range(TC):
                    last = nc.vector.bn_stats(st6[:, t, :], tile(t))
                    if t < TC - 1:
                        steps[0] += 1
                        last.then_inc(ln_step, 1)
                link(last)
                for t in range(TC):
                    last = nc.vector.bn_aggr(mv[:, n % 2, t, :], st6[:, t, :])
                    if t < TC - 1:
                        steps[0] += 1
                        last.then_inc(ln_step, 1)
                link(last)
                nc.vector.tensor_scalar(ve[:, n % 2, :], mv[:, n % 2, :, 1], EPS, None, ALU.add).then_inc(var_ready, 1)

            def scale(n, tile, put, done):
                dve.wait_ge(var_ready, n + 1)
                dve.wait_ge(rsqrt_ready, n + 1)
                r = rs[:, n % 2, :]
                link(nc.vector.scalar_tensor_tensor(ta[:, :], r, -0.5, r, ALU.mult, ALU.mult))
                link(nc.vector.tensor_tensor(tb[:, :], ta[:, :], ve[:, n % 2, :], ALU.mult))
                link(nc.vector.scalar_tensor_tensor(ta[:, :], tb[:, :], 1.5, r, ALU.add, ALU.mult))
                for t in range(TC):
                    last = nc.vector.tensor_scalar(put(t), tile(t), mv[:, n % 2, t, 0:1], ta[:, t:t + 1],
                                                   ALU.subtract, ALU.mult)
                    if t < TC - 1:
                        steps[0] += 1
                        last.then_inc(ln_step, 1)
                last.then_inc(done, 1)

            def stream_entry(i, n, mrow_seen):
                m = STREAM[i]
                bank = MB[i % M_RING]
                dve.wait_ge(m_ready, n + 1)
                if m[0] == "turn":
                    slot = (m[1] + 1) % 2
                    if mrow_seen is not None:
                        dve.wait_ge(mrow[slot], mrow_seen)
                    nc.vector.tensor_copy(mT[:, slot, :], bank[0:3 * HG * TC, 0:P // 2].bitcast(BF16))\
                      .then_inc(m_done, 1)
                    return
                _, c, t, j, kc = m
                w = m_width(m)
                if kc < c:
                    nc.vector.tensor_reduce(pm[:, c, TC * j + t, kc:kc + 1], bank[:, 0:w], AX.X, ALU.max)\
                      .then_inc(m_done, 1)
                else:
                    if not (isinstance(n, int) and n < M_RING):
                        dve.wait_ge(m_done, n + 1 - m_free(i))
                    dve.sem_inc(dve_passed, 1)
                    nc.vector.tensor_tensor_reduce(
                        out=junk[:, i % M_RING, 0:w], in0=bank[:, 0:w], in1=tri[:, CW - w:CW], scale=1.0, scalar=NEG,
                        op0=ALU.add, op1=ALU.max, accum_out=pm[:, c, TC * j + t, kc:kc + 1]).then_inc(m_done, 1)

            def fold(c, n):
                dve.wait_ge(m_done, n + 1)
                nc.vector.tensor_reduce(mr[:, :], pm[:, c, :, :], AX.X, ALU.max, negate=True).then_inc(folded, 1)

            def x_moments(c):
                dve.wait_ge(x_loaded[c], 16)
                moments(c, lambda t: x_sb[:, TC * c + t, :])

            x_moments(0)
            for c in range(NC):
                if c >= 1:
                    dve.wait_ge(xh_ready, c)
                if c + 1 < NC:
                    x_moments(c + 1)
                if c >= 2:
                    dve.wait_ge(pro_ready, 1 + PRO.index(("T", c - 2, 1)))
                scale(c, lambda t: x_sb[:, TC * c + t, :], lambda t: xh[:, c % 2, t, :], xh_ready)
            dve.wait_ge(id_loaded, 16)
            nc.vector.tensor_copy(id_b[:, :], id_f[:, :]).then_inc(consts_ready, 1)
            nc.vector.memset(mparts[:, :, :, :], 0.0).then_inc(consts_ready, 1)
            link(nc.vector.memset(pm[:, :, :, :], NEG))
            dve.wait_ge(tri_loaded, 16)
            for i in range(LEAD):
                stream_entry(i, i, None)
                if i in M_END:
                    fold(M_END.index(i), i)

            with dve.Fori(0, NG // 2) as it:
                for u in range(2):
                    g = 2 * it + u
                    m_base = LEAD + SN * g
                    for s in range(SS):
                        for i, following in BODY[s]:
                            seen = None
                            if STREAM[i][0] == "turn":
                                c = STREAM[i][1]
                                uses = {2: 1, 3: 1, 0: 2, 1: 2}[c]
                                seen = 48 * (2 * g + uses)
                            stream_entry(i, m_base + stream_place(i, following), seen)
                            if i in M_END:
                                fold(M_END.index(i), m_base + stream_place(i, following))

            dve.wait_ge(den_loaded, 16 * NC)
            nc.vector.reciprocal(rden_c[:, :], den_c[:, :]).then_inc(rden_ready, 1)

            def attn(c):
                dve.wait_ge(at_loaded[c % 2], 16 * 2 * FC * (c // 2 + 1))
                if c >= 1:
                    dve.wait_ge(wo_ready, 2 * c)
                nc.vector.tensor_tensor(at[:, :, :], nm[:, c % 2, :, :], rd[:, c % 2, :, :], ALU.mult)\
                  .then_inc(at_ready, 1)

            def residual(c):
                for h in range(2):
                    dve.wait_ge(wo_ready, 2 * c + h + 1)
                    rows = x_sb[:, TC * c + 2 * h:TC * c + 2 * h + 2, :].rearrange("p t d -> p (t d)")
                    nc.vector.tensor_tensor(rows, PB[h][:, :], rows, ALU.add).then_inc(x1_ready, 1)
                dve.wait_ge(x1_ready, 2 * (c + 1))
                if c >= 1:
                    dve.wait_ge(xt2_psum, 2 * c)
                moments(NC + c, lambda t: x_sb[:, TC * c + t, :])
                scale(NC + c, lambda t: x_sb[:, TC * c + t, :], lambda t: xh2[:, t, :], xh2_ready)

            def route(c):
                dve.wait_ge(lg_ready, c + 1)
                nc.vector.tensor_copy(lg[:, :, :], MB[0][:, 0:TC * E].rearrange("p (t e) -> p t e", e=E))\
                  .then_inc(lg_read, 1)
                dve.wait_ge(lg_read, c + 1)
                for t in range(TC):
                    link(nc.vector.max(top[:, t, :], lg[:, t, :]))
                for t in range(TC):
                    link(nc.vector.max_index(idx[:, t, :], top[:, t, :], lg[:, t, :]))
                nc.vector.tensor_tensor(gd[:, :], top[:, :, 1], top[:, :, 0], ALU.subtract).then_inc(gd_ready, 1)
                link(nc.vector.tensor_copy(idf[:, :, :], idx[:, :, 0:2]))
                dve.wait_ge(ge_ready, c + 1)
                link(nc.vector.tensor_scalar(gs[:, :], ge[:, :], 1.0, None, ALU.add))
                link(nc.vector.reciprocal(gw[:, :, 0], gs[:, :]))
                link(nc.vector.tensor_tensor(gw[:, :, 1], gw[:, :, 0], ge[:, :], ALU.mult))
                for t in range(TC):
                    for n, dst in ((0, g1), (1, g2)):
                        steps[0] += 1
                        nc.vector.tensor_scalar(dst[:, t, :], iota[:, :], idf[:, t, n:n + 1], gw[:, t, n:n + 1],
                                                ALU.is_equal, ALU.mult).then_inc(ln_step, 1)
                dve.wait_ge(ln_step, steps[0])
                nc.vector.tensor_tensor(gates[:, c % 2, :, :], g1[:, :, :], g2[:, :, :], ALU.add)\
                  .then_inc(gates_ready, 1)
                dve.wait_ge(gates_ready, c + 1)

            def begin(c):
                if c >= 2:
                    dve.wait_ge(y_stored[c % 2], 16 * TC * (c // 2))
                for h in range(2):
                    dve.wait_ge(gb_ready, 2 * c + h + 1)
                    rows = slice(2 * h, 2 * h + 2)
                    nc.vector.tensor_tensor(
                        yb[:, c % 2, rows, :].rearrange("p t d -> p (t d)"), PB[h][:, :],
                        x_sb[:, TC * c + 2 * h:TC * c + 2 * h + 2, :].rearrange("p t d -> p (t d)"), ALU.add)\
                        .then_inc(yb_ready, 1)
                dve.wait_ge(yb_ready, 2 * (c + 1))

            def combine(c, t):
                y = yb[:, c % 2, t, :]
                for e2 in range(E // 2):
                    n = (TC * c + t) * (E // 2) + e2
                    dve.wait_ge(ex_ready, n + 1)
                    for h in range(2):
                        e = 2 * e2 + h
                        ins = nc.vector.scalar_tensor_tensor(
                            out=y, in0=ring4[n % 4][:, F * h:F * (h + 1)], scalar=gates[:, c % 2, t, e:e + 1],
                            in1=y, op0=ALU.mult, op1=ALU.add)
                        if h == 0:
                            link(ins)
                        else:
                            ins.then_inc(ex_done, 1)
                            dve.wait_ge(ex_done, n + 1)

            attn(0)
            dve.wait_ge(xb_ready, NC)
            dve.wait_ge(iota_ready, E)
            residual(0)
            route(0)
            for c in range(NC):
                more = c + 1 < NC
                if more:
                    attn(c + 1)
                begin(c)
                combine(c, 0)
                combine(c, 1)
                if more:
                    residual(c + 1)
                combine(c, 2)
                combine(c, 3)
                if more:
                    route(c + 1)

        @block.gpsimd
        def _(pool):
            steps = [0]

            def link(ins):
                steps[0] += 1
                ins.then_inc(vg_set, 1)
                pool.wait_ge(vg_set, steps[0])

            def split_maxima(c, number):
                split = mparts[:, (c + 1) % 2, :, :]
                pool.wait_ge(folded, number)

                pool.sem_inc(pool_passed, 1)

                def step(k, ins):
                    ins.then_inc(mpost_step, 1)
                    pool.wait_ge(mpost_step, (number - 1) * 3 + k)
                    pool.sem_inc(pool_passed, 1)

                step(1, nc.gpsimd.tensor_copy(split[:, 0, :], mr[:, :]))
                step(2, nc.gpsimd.tensor_tensor(mx[:, :], mr[:, :], split[:, 0, :], ALU.subtract))
                step(3, nc.gpsimd.tensor_copy(split[:, 1, :], mx[:, :]))
                nc.gpsimd.tensor_tensor(split[:, 2, :], mx[:, :], split[:, 1, :], ALU.subtract)\
                    .then_inc(mparts_ready, 1)

            def split_pair(v):
                for k in (v, v + 1):
                    pool.wait_ge(high_ready, k + 1)
                    nc.gpsimd.tensor_tensor(r1[:, k % 2, :], qf[:, k % 2, :], parts[:, k % 2, 0, :], ALU.subtract)\
                        .then_inc(rest_ready, 1)
                for k in (v, v + 1):
                    pool.wait_ge(mid_ready, k + 1)
                    nc.gpsimd.tensor_tensor(parts[:, k % 2, 2, :], r1[:, k % 2, :], parts[:, k % 2, 1, :],
                                            ALU.subtract).then_inc(low_ready, 1)

            def place_values(b, col):
                src = V[:, :, bass.ds(col, HG * DH)].rearrange("p k (j d) -> p k j d", d=DH)
                bias = bv_sb[:, bass.ds(col, HG * DH)].rearrange("p (j d) -> p j d", d=DH)\
                    .unsqueeze(1).broadcast_to([P, NT, HG, DH])
                pool.sem_inc(pool_passed, 1)
                nc.gpsimd.tensor_tensor(Vg[b][:, :, :, 0:DH], src, bias, ALU.add).then_inc(vg_ready, 1)

            link(nc.gpsimd.memset(neg_half[:, :], -0.5))
            for b in range(2):
                link(nc.gpsimd.memset(Vg[b][:, :, :, DH:VW], 0.0))
                link(nc.gpsimd.memset(Vg[b][:, :, :, DH:DH + 1], 1.0))
            nc.gpsimd.memset(ones[:, :], 1.0).then_inc(ones_ready, 1)

            def rsqrt(n):
                pool.wait_ge(var_ready, n + 1)
                nc.gpsimd.tensor_tensor(rs[:, n % 2, :], ve[:, n % 2, :], neg_half[:, :], ALU.pow)\
                    .then_inc(rsqrt_ready, 1)

            for c in range(NC):
                rsqrt(c)
            v = maxima = 0
            for item in DONE:
                if item[0] == "QK" and item[3] == 1:
                    split_pair(v)
                    v += 2
                elif item == ("V", NT // 2 - 1):
                    pool.wait_ge(biases_loaded, 32)
                    pool.wait_ge(pro_done, 1 + PRO.index(item))
                    place_values(0, 0)
                elif item[0] == "M" and item[1] in M_END:
                    maxima += 1
                    split_maxima(M_END.index(item[1]), maxima)

            with pool.Fori(0, NG // 2) as it:
                for u in range(2):
                    g = 2 * it + u
                    m_base = LEAD + SN * g
                    pool.wait_ge(pv_done, P_SLOTS + SS * g)
                    pool.sem_inc(pool_passed, 1)
                    place_values(1 - u, (2 * it + 1) * (HG * DH) if u == 0 else (1 - it) * (2 * HG * DH))
                    for s in range(SS):
                        c, _ = STEPS[s]
                        if diag(s) is not None:
                            pool.wait_ge(exp_done, g * (2 * SS) + (2 * s + 4))
                            pool.sem_inc(pool_passed, 1)
                            block_ = probs[:, s % P_SLOTS, :, 0:P]
                            nc.gpsimd.affine_select(out=block_, in_=block_, compare_op=ALU.is_ge, fill=0.0, base=0,
                                                    pattern=[[0, HG], [1, P]], channel_multiplier=-1)\
                                .then_inc(mask_done, 1)
                        for i, following in BODY[s]:
                            if i in M_END:
                                place = stream_place(i, following)
                                split_maxima(M_END.index(i), NC * g + turn_number(place))

            pool.wait_ge(xh_ready, NC)
            for c in range(NC):
                rows = x_sb[:, TC * c:TC * (c + 1), :]
                nc.gpsimd.tensor_tensor(rows, rows, bo_sb[:, :].unsqueeze(1).broadcast_to([P, TC, D]), ALU.add)\
                    .then_inc(xb_ready, 1)
                if c == 0:
                    for e in range(E):
                        nc.gpsimd.memset(iota[:, e:e + 1], float(e)).then_inc(iota_ready, 1)
            for c in range(NC):
                rsqrt(NC + c)


def kernel(L0_attn_X, L0_attn_Wq, L0_attn_bq, L0_attn_Wk, L0_attn_bk, L0_attn_Wv, L0_attn_bv, L0_attn_Wo, L0_attn_bo,
           L0_ffn_Wr, L0_ffn_We, L0_ffn_be):
    import numpy as np
    import concourse.bacc as bacc
    from concourse.bass_utils import run_bass_kernel_spmd

    def lay(a):
        return np.ascontiguousarray(a)

    def by_group(a):
        a = np.asarray(a)
        return lay(np.swapaxes(a.reshape(a.shape[:-1] + (NG, HG, DH)), -1, -2).reshape(a.shape))

    arrays = {
        "X": lay(np.asarray(L0_attn_X).reshape(S, D)),
        "WqT": by_group(np.asarray(L0_attn_Wq).T), "WkT": by_group(np.asarray(L0_attn_Wk).T),
        "WvT": lay(np.asarray(L0_attn_Wv).T), "WoT": lay(np.asarray(L0_attn_Wo).T),
        "bq": by_group(L0_attn_bq), "bk": by_group(L0_attn_bk), "bv": lay(L0_attn_bv), "bo": lay(L0_attn_bo),
        "Wr": lay(L0_ffn_Wr), "We": lay(L0_ffn_We), "be": lay(L0_ffn_be),
        "ident": np.eye(P, dtype=np.float32),
        "trimask": np.where(np.arange(CW)[None, :] - (CW - P) <= np.arange(P)[:, None], 0.0, NEG).astype(np.float32),
    }
    nc = bacc.Bacc("TRN2", target_bir_lowering=False, num_devices=1)
    args, feed = {}, {}
    for name, a in arrays.items():
        feed["in_" + name] = a
        args[name] = nc.dram_tensor("in_" + name, a.shape, mybir.dt.from_np(a.dtype), kind="ExternalInput").ap()
    shape, dtype = (S, D), np.dtype("float32")
    out = nc.dram_tensor("out_y", shape, mybir.dt.from_np(dtype), kind="ExternalOutput").ap()
    build_program(nc, out=out, **args)
    r = run_bass_kernel_spmd(nc, [feed], core_ids=[0])
    return r.results[0]["out_y"].reshape(1, S, D)
```

```python
from contextlib import ExitStack

import concourse.bass as bass
from concourse import mybir
from concourse.alu_op_type import AluOpType as ALU

F32 = mybir.dt.float32
BF16 = mybir.dt.bfloat16
U32 = mybir.dt.uint32
ACT = mybir.ActivationFunctionType
AX = mybir.AxisListType

P = 128
S = 2048
D = 256
H = 16
DH = D // H
E = 8
F = 256
EPS = 1e-5
NEG = -1e30

FC = D // P
NT = S // P
CW = 512
NC = S // CW
TC = CW // P
HG = 4
NG = H // HG
PARTS = 3
RUNS = [(0, 3, 0), (1, 2, 3), (2, 1, 5)]
TERMS = sum(copies for _, copies, _ in RUNS)
SR = TERMS * DH
SX = SR + 3
VW = 32

M_RING = 3
M_LAG = 8


def max_stream():
    out = []
    for c in range(NC):
        blocks = [("max", c, t, j, kc) for t in range(TC) for j in range(HG) for kc in range(c + 1)]
        out += blocks[:M_LAG] + [("turn", (c - 1) % NC)] + blocks[M_LAG:]
    return out


STREAM = max_stream()
SN = len(STREAM)
M_END = [max(i for i, m in enumerate(STREAM) if m[0] == "max" and m[1] == c) for c in range(NC)]
LEAD = 92


def m_free(i):
    return M_RING if i >= SN % M_RING else SN % M_RING


def m_width(m):
    if m[0] == "turn":
        return P
    _, c, t, _, kc = m
    return CW if kc < c else (t + 1) * P


STEPS = [(c, kt) for c in range(NC) for kt in range(TC * (c + 1))]
SS = len(STEPS)
C_END = [max(s for s, (c, _) in enumerate(STEPS) if c == cc) for cc in range(NC)]
PV_LAG = 2
P_SLOTS = 4
DIAGS = NC * TC


def diag(s):
    c, kt = STEPS[s]
    return kt - TC * c if kt >= TC * c else None


def step_off(s):
    return P * (diag(s) or 0)


ORDER = [(i, False) for i in range(LEAD, SN)] + [(i, True) for i in range(LEAD)]
LAST_M_STEP = 19
LAST_TURN = (M_LAG, True)


def body_stream(order, last_step):
    m_total = sum(m_width(STREAM[i]) for i, _ in order)
    s_total = sum(CW - step_off(s) for s in range(last_step + 1))
    out, at, m_cols, s_cols = [], 0, 0, 0
    for s in range(SS):
        s_cols += CW - step_off(s)
        mine = []
        while at < len(order) and (m_cols < m_total * s_cols / s_total or s == last_step):
            mine.append(order[at])
            m_cols += m_width(STREAM[order[at][0]])
            at += 1
        out.append(mine)
    return out


BODY = body_stream(ORDER, SS - 1)
LAST_BODY = body_stream(ORDER[:SN - LEAD] + [LAST_TURN], LAST_M_STEP)


def m_place(entry, last):
    return SN - LEAD if last and entry == LAST_TURN else ORDER.index(entry)


TURNS_BEFORE = sum(m[0] == "turn" for m in STREAM[1 + M_LAG:LEAD])


def turn_number(entry):
    return 1 + TURNS_BEFORE + sum(STREAM[i][0] == "turn" for i, _ in ORDER[:ORDER.index(entry)])


O_STEP = [min(C_END[c] + PV_LAG + 1, SS - 1) for c in range(NC)]
DEN_STEP = [O_STEP[c] + 2 for c in range(NC - 1)]
RDEN_STEP = [DEN_STEP[c] + 2 for c in range(NC - 1)]
XB_STEP = 12
PROJECT_STEP = 24
TURN_STEP = 29
LOGITS_STEP = 31
GATE_STEP = 33


def build_program(nc, X, WqT, WkT, WvT, WoT, bq, bk, bv, bo, Wr, We, be, ident, trimask, out):
    ctx = ExitStack()
    with ctx:
        def sb(name, shape, dt=F32):
            return ctx.enter_context(nc.sbuf_tensor(name, shape, dt))

        def sem(name):
            return ctx.enter_context(nc.semaphore(name))

        qk_d = nc.dram_tensor("qk_parts", [2, NG, NC, PARTS, DH, HG * CW], BF16, kind="Internal").ap()
        o_d = nc.dram_tensor("attn_sums", [NC, H, VW, CW], F32, kind="Internal").ap()
        rden_d = nc.dram_tensor("attn_rden", [NC, H, CW], F32, kind="Internal").ap()

        x_sb = sb("x_sb", [P, NT, D])
        wq, wk, wv, wo = (sb(n, [P, FC, D]) for n in ("wq", "wk", "wv", "wo"))
        we_sb = sb("we_sb", [P, FC, E * F])
        wr_sb = sb("wr_sb", [P, FC, E])
        be_sb = sb("be_sb", [E, F])
        bv_sb = sb("bv_sb", [P, D])
        bo_sb = sb("bo_sb", [P, D])
        bqk = sb("bqk", [P, 2, FC])
        bqk_half = sb("bqk_half", [P, 2, FC])
        id_f = sb("id_f", [P, P])
        id_b = sb("id_b", [P, P], BF16)
        tri = sb("tri", [P, CW])
        iota = sb("iota", [P, E])
        ones = sb("ones", [3, CW], BF16)
        parts = sb("parts", [P, 2, PARTS, CW], BF16)
        V = sb("V", [P, NT, D])
        Vg = [sb(f"Vg{b}", [P, NT, HG, VW]) for b in range(2)]
        Qo = [sb(f"Qo{b}", [P, NC, HG, CW], BF16) for b in range(2)]
        Ko = [sb(f"Ko{b}", [P, NC, HG, CW], BF16) for b in range(2)]
        probs = sb("probs", [P, P_SLOTS, HG, CW])
        O_sb = sb("O_sb", [P, 2, CW])
        junk = sb("junk", [P, M_RING, CW], BF16)
        pm = sb("pm", [P, NC, HG * TC, NC])
        mx = sb("mx", [P, HG * TC])
        mr = sb("mr", [P, HG * TC])
        mparts = sb("mparts", [P, 2, 5, HG * TC], BF16)
        mT = sb("mT", [3 * HG * TC, 2, P], BF16)
        st6 = sb("st6", [P, TC, 6])
        mv = sb("mv", [P, 2, TC, 2])
        ve = sb("ve", [P, 2, TC])
        rs = sb("rs", [P, 2, TC])
        ta = sb("ta", [P, TC])
        neg_half = sb("neg_half", [P, TC])
        tb = sb("tb", [P, TC])
        den_c = sb("den_c", [P, H * S // P])
        rden_c = sb("rden_c", [P, H * S // P])
        lg = sb("lg", [P, TC, E])
        top = sb("top", [P, TC, 8])
        idx = sb("idx", [P, TC, 8], U32)
        idf = sb("idf", [P, TC, 2])
        gd = sb("gd", [P, TC])
        ge = sb("ge", [P, TC])
        gs = sb("gs", [P, TC])
        gw = sb("gw", [P, TC, 2])
        g1 = sb("g1", [P, TC, E])
        g2 = sb("g2", [P, TC, E])
        gT = sb("gT", [E, CW])
        gates = sb("gates", [P, 2, TC, E])

        q1f = Qo[1][:, :, :, :].rearrange("p c j w -> p (c j w)").bitcast(F32)
        xT = Ko[1][:, :, :, :].rearrange("p c j w -> p (c j w)").bitcast(F32).rearrange("p (f s) -> p f s", f=FC)
        xh = q1f[:, 0:2 * TC * D].rearrange("p (b t d) -> p b t d", b=2, t=TC)
        qf = q1f[:, 2048:3072].rearrange("p (b w) -> p b w", b=2)
        r1 = q1f[:, 3072:4096].rearrange("p (b w) -> p b w", b=2)
        q0f = Qo[0][:, :, :, :].rearrange("p c j w -> p (c j w)").bitcast(F32)
        k0f = Ko[0][:, :, :, :].rearrange("p c j w -> p (c j w)").bitcast(F32)
        nm = q0f[:, 0:2048].rearrange("p (b f w) -> p b f w", b=2, f=FC)
        rd = q0f[:, 2048:4096].rearrange("p (b f w) -> p b f w", b=2, f=FC)
        at = k0f[:, 0:1024].rearrange("p (f w) -> p f w", f=FC)
        xh2 = k0f[:, 1024:2048].rearrange("p (t d) -> p t d", t=TC)
        xT2 = k0f[:, 2048:4096].rearrange("p (b f w) -> p b f w", b=2, f=FC)
        yb = V[:, 0:2 * TC, :].rearrange("p (b t) d -> p b t d", b=2)

        ST = [ctx.enter_context(nc.psum_tensor(f"ST{i}", [P, 2, CW], F32)) for i in range(2)]
        MB = [ctx.enter_context(nc.psum_tensor(f"MB{i}", [P, CW], F32)) for i in range(M_RING)]
        OB = ctx.enter_context(nc.psum_tensor("OB", [P, CW], F32))
        XB = [MB[0], MB[1]]
        PB = [MB[1], MB[2]]
        ring4 = [ST[0][:, 0, :], ST[0][:, 1, :], ST[1][:, 0, :], ST[1][:, 1, :]]

        x_loaded = [sem(f"x_loaded{c}") for c in range(NC)]
        id_loaded, w_loaded, v_loaded, e_loaded = sem("id_loaded"), sem("w_loaded"), sem("v_loaded"), sem("e_loaded")
        tri_loaded, biases_loaded = sem("tri_loaded"), sem("biases_loaded")
        consts_ready = sem("consts_ready")
        var_ready, rsqrt_ready = sem("var_ready"), sem("rsqrt_ready")
        ln_step = sem("ln_step")
        xh_ready = sem("xh_ready")
        pro_ready, pro_done = sem("pro_ready"), sem("pro_done")
        bias_ready = sem("bias_ready")
        high_ready, rest_ready, mid_ready, low_ready = (
            sem(n) for n in ("high_ready", "rest_ready", "mid_ready", "low_ready"))
        parts_stored = [[sem(f"parts_stored{i}{half}") for half in range(2)] for i in range(2)]
        vg_set, vg_ready = sem("vg_set"), sem("vg_ready")
        ones_ready, ones_placed = sem("ones_ready"), [sem(f"ones_placed{b}") for b in range(2)]
        xb_ready, iota_ready = sem("xb_ready"), sem("iota_ready")
        first_ops = [sem(f"first_ops{c}") for c in range(NC)]
        ops_loaded = [sem(f"ops_loaded{b}") for b in range(2)]
        m_ready, m_done = sem("m_ready"), sem("m_done")
        folded = sem("folded")
        mpost_step = sem("mpost_step")
        mparts_ready = sem("mparts_ready")
        mrow = [sem(f"mrow{i}") for i in range(2)]
        st_ready, exp_done = sem("st_ready"), sem("exp_done")
        mask_done, pv_done = sem("mask_done"), sem("pv_done")
        o_out = sem("o_out")
        o_stored = [sem(f"o_stored{i}") for i in range(2)]
        den_loaded = [sem(f"den_loaded{c}") for c in range(NC)]
        rden_ready, rden_stored = sem("rden_ready"), sem("rden_stored")
        at_loaded = [sem(f"at_loaded{i}") for i in range(2)]
        at_ready, wo_ready, x1_ready = sem("at_ready"), sem("wo_ready"), sem("x1_ready")
        xh2_ready, xt2_psum, xt2_ready = sem("xh2_ready"), sem("xt2_psum"), sem("xt2_ready")
        lg_ready, gd_ready, ge_ready, gates_ready = sem("lg_ready"), sem("gd_ready"), sem("ge_ready"), sem("gates_ready")
        lg_read = sem("lg_read")
        ex_ready, ex_done = sem("ex_ready"), sem("ex_done")
        gt_psum, gt_ready, gb_ready, yb_ready = sem("gt_psum"), sem("gt_ready"), sem("gb_ready"), sem("yb_ready")
        y_stored = [sem(f"y_stored{i}") for i in range(2)]
        dve_passed, pool_passed, sp_passed = sem("dve_passed"), sem("pool_passed"), sem("sp_passed")

        BANK_PARTS = {"T": 1, "QK": 2, "V": 2}
        M_AFTER = 6

        def prologue_plan():
            def qk(c, f):
                return [("QK", c, f, side) for side in range(2)]

            def t(c):
                return [("T", c, f) for f in range(FC)]

            def parts_of(banks):
                return [(item, k) for item in banks for k in range(BANK_PARTS[item[0]])]

            head = parts_of(t(0) + qk(0, 0) + [("V", 0)] + t(1) + qk(1, 0) + [("V", 1)] + t(2) + [("V", 2)])
            rest = parts_of(qk(2, 0) + t(3) + qk(3, 0) + [("V", 3)] + qk(0, 1) + [("V", 4), ("V", 5)] + qk(1, 1)
                            + [("V", 6), ("V", 7)] + qk(2, 1) + qk(3, 1))
            plan, at = list(head), 0
            for n in range(LEAD):
                while at < len(rest) and at * (LEAD - M_AFTER) <= n * len(rest):
                    plan.append(rest[at])
                    at += 1
                plan.append((("M", n), 0))
            return plan

        PLAN = prologue_plan()
        DONE = [item for item, part in PLAN if part == BANK_PARTS.get(item[0], 1) - 1]
        PRO = [item for item in DONE if item[0] != "M"]
        DW = H * CW // P
        M_CHUNK_START = [0] + [e + 1 for e in M_END[:-1]]

        block = ctx.enter_context(nc.Block())

        @block.sync
        def _(sp):
            xv = X.rearrange("(c t p) d -> c p t d", t=TC, p=P)

            def load_x(c):
                sp.dma_start(x_sb[:, TC * c:TC * (c + 1), :], xv[c]).then_inc(x_loaded[c], 16)

            for i in range(2):
                sp.sem_inc(o_stored[i], 16)
            load_x(0)
            sp.dma_start(id_f[:, :], ident).then_inc(id_loaded, 16)
            sp.dma_start(wq[:, :, :], WqT.rearrange("(a p) n -> p a n", p=P)).then_inc(w_loaded, 16)
            sp.dma_start(wk[:, :, :], WkT.rearrange("(a p) n -> p a n", p=P)).then_inc(w_loaded, 16)
            load_x(1)
            for side, b in enumerate((bq, bk)):
                sp.dma_start(bqk[:, side, :], b.rearrange("(a p) -> p a", p=P),
                             allow_slow_non_contiguous=True).then_inc(w_loaded, 16)
            sp.dma_start(wv[:, :, :], WvT.rearrange("(a p) n -> p a n", p=P)).then_inc(v_loaded, 16)
            for c in range(2, NC):
                load_x(c)
            sp.dma_start(tri[:, :], trimask).then_inc(tri_loaded, 16)
            sp.dma_start(bv_sb[:, :], bv.partition_broadcast(P)).then_inc(biases_loaded, 16)
            sp.dma_start(bo_sb[:, :], bo.partition_broadcast(P)).then_inc(biases_loaded, 16)

            def store_parts(v, c, f, side):
                sp.wait_ge(low_ready, v + 1)
                for half in range(2):
                    dst = qk_d[side, 2 * f + half, c].rearrange("a d (j q) -> (d j) a q", q=CW)
                    sp.dma_start(dst, parts[P // 2 * half:P // 2 * (half + 1), v % 2, :, :])\
                      .then_inc(parts_stored[v % 2][half], 16)

            def load_first(c):
                for slot in range(2):
                    sp.wait_ge(parts_stored[slot][0], 16 * (c + 1))
                for part, copies, block_ in RUNS:
                    rows = slice(DH * block_, DH * (block_ + copies))
                    sp.dma_start(Qo[0][rows, c, :, :], qk_d[0, 0, c, part].unsqueeze(0)
                                 .broadcast_to([copies, DH, HG * CW])).then_inc(first_ops[c], 16)
                    sp.dma_start(Ko[0][rows, c, :, :], qk_d[1, 0, c, 0:copies]).then_inc(first_ops[c], 16)

            def load_group(b, group):
                for part, copies, block_ in RUNS:
                    rows = slice(DH * block_, DH * (block_ + copies))
                    for copy in range(copies):
                        first = DH * (block_ + copy)
                        sp.dma_start(Qo[b][first:first + DH, :, :, :],
                                     qk_d[0, bass.ds(group, 1), :, part].rearrange("g c d q -> d (g c) q"))\
                          .then_inc(ops_loaded[b], 16)
                    sp.dma_start(Ko[b][rows, :, :, :], qk_d[1, bass.ds(group, 1), :, 0:copies]
                                 .rearrange("g c a d q -> (a d) (g c) q")).then_inc(ops_loaded[b], 16)

            def place_row(b, c, slot, m_seen):
                sp.wait_ge(m_done, m_seen)
                for n in range(3):
                    sp.dma_start(Qo[b][SR + n:SR + n + 1, c, :, :], mT[HG * TC * n:HG * TC * (n + 1), slot, :])\
                      .then_inc(mrow[slot], 16)

            def place_ones(b):
                sp.wait_ge(ones_ready, 1)
                sp.dma_start(Ko[b][SR:SX, :, :, :].rearrange("p c j w -> p (c j) w"),
                             ones[:, :].unsqueeze(1).broadcast_to([3, HG * NC, CW])).then_inc(ones_placed[b], 16)

            v = 0
            place_ones(0)
            for item in DONE:
                if item[0] == "QK":
                    _, c, f, side = item
                    store_parts(v, c, f, side)
                    if f == 0 and side == 1:
                        load_first(c)
                    v += 1
                elif item[0] == "M" and STREAM[item[1]][0] == "turn" and item[1] > M_LAG:
                    c = STREAM[item[1]][1]
                    place_row(0, c, (c + 1) % 2, item[1] + 1)
            sp.dma_start(wo[:, :, :], WoT.rearrange("(a p) n -> p a n", p=P)).then_inc(e_loaded, 16)
            sp.dma_start(wr_sb[:, :, :], Wr.rearrange("(a p) e -> p a e", p=P)).then_inc(e_loaded, 16)
            for e in range(E):
                sp.dma_start(we_sb[:, :, F * e:F * (e + 1)], We[e].rearrange("(a p) f -> p a f", p=P))\
                  .then_inc(e_loaded, 16)
            sp.dma_start(be_sb[:, :], be).then_inc(e_loaded, 16)
            for slot in range(2):
                for half in range(2):
                    sp.wait_ge(parts_stored[slot][half], 16 * 2 * NC)

            sp.wait_ge(st_ready, 1)
            place_ones(1)

            def load_den(c):
                sp.wait_ge(o_stored[c % 2], 16 + 16 * ((NG - 1) * (NC // 2) + c // 2 + 1))
                sp.dma_start(den_c[:, DW * c:DW * (c + 1)], o_d[c, :, DH, :].rearrange("h (a w) -> h a w", w=DW))\
                  .then_inc(den_loaded[c], 16)

            def load_attn(c):
                sp.wait_ge(rden_ready, c + 1)
                sp.dma_start(rden_d[c].rearrange("h (a w) -> (h a) w", w=DW), rden_c[:, DW * c:DW * (c + 1)])\
                  .then_inc(rden_stored, 16)
                if c >= 2:
                    sp.wait_ge(at_ready, c - 1)
                hs = P // DH
                for f in range(FC):
                    sp.dma_start(nm[:, c % 2, f, :], o_d[c, hs * f:hs * (f + 1), 0:DH, :])\
                      .then_inc(at_loaded[c % 2], 16)
                sp.wait_ge(rden_stored, 16 * (c + 1))
                for f in range(FC):
                    src = rden_d[c, hs * f:hs * (f + 1), :]
                    sp.dma_start(rd[:, c % 2, f, :], src.unsqueeze(1).broadcast_to([hs, DH, CW]))\
                      .then_inc(at_loaded[c % 2], 16)

            def group(g, u, last=False):
                m_base = LEAD + SN * g
                sp.wait_ge(st_ready, g * (2 * SS) + 1)
                if not last:
                    sp.sem_inc(sp_passed, 1)
                    load_group(1 - u, g + 1)
                for s in range(SS):
                    for entry in (LAST_BODY if last else BODY)[s]:
                        i, following = entry
                        if STREAM[i][0] == "turn":
                            c = STREAM[i][1]
                            b = 1 - u if following and i > M_LAG else u
                            place_row(b, c, (c + 1) % 2, m_base + (m_place(entry, last) + 1))
                    for c in range(NC):
                        if s == O_STEP[c]:
                            sp.wait_ge(o_out, g * NC + (c + 2))
                            sp.dma_start(o_d[c, bass.ds(g * HG, HG), :, :].rearrange("h d q -> (h d) q"),
                                         O_sb[:, c % 2, :]).then_inc(o_stored[c % 2], 16)
                    if last and s in DEN_STEP:
                        load_den(DEN_STEP.index(s))
                    if last and s in RDEN_STEP:
                        load_attn(RDEN_STEP.index(s))

            with sp.Fori(0, NG // 2 - 1) as it:
                for u in range(2):
                    group(2 * it + u, u)
            group(NG - 2, 0)
            group(NG - 1, 1, last=True)

            load_den(NC - 1)
            load_attn(NC - 1)
            ov = out.rearrange("(n t p) d -> n p t d", t=2, p=P)
            for n in range(NT // 2):
                c = n // 2
                sp.wait_ge(yb_ready, n + 1)
                sp.dma_start(ov[n], yb[:, c % 2, 2 * (n % 2):2 * (n % 2) + 2, :]).then_inc(y_stored[c % 2], 16)
            for i in range(2):
                sp.wait_ge(y_stored[i], 16 * NT // 4)

        @block.tensor
        def _(pe):
            def stream_entry(i, b, n, turn, ring=None):
                m = STREAM[i]
                free = m_free(i) if ring is None else M_RING
                ring = i % M_RING if ring is None else ring
                if not (isinstance(n, int) and n < M_RING):
                    pe.wait_ge(m_done, n + 1 - free)
                bank = MB[ring]
                if m[0] == "turn":
                    if not (isinstance(turn, int) and turn == 0):
                        pe.wait_ge(mparts_ready, turn)
                    slot = (m[1] + 1) % 2
                    nc.tensor.transpose(bank[0:5 * HG * TC, 0:P // 2].bitcast(BF16),
                                        mparts[:, slot, :, :].rearrange("p a m -> p (a m)"), id_b[:, :])\
                      .then_inc(m_ready, 1)
                    return
                _, c, t, j, kc = m
                w = m_width(m)
                nc.tensor.matmul(bank[:, 0:w], Qo[b][0:SR, c, j, P * t:P * (t + 1)],
                                 Ko[b][0:SR, kc, j, 0:w], start=True, stop=True).then_inc(m_ready, 1)

            def pro_bank(n, item, part):
                if n >= 4 and part == 0:
                    pe.wait_ge(pro_done, n - 3)
                bank = ring4[n % 4]
                if item[0] == "T":
                    _, c, f = item
                    if f == 0:
                        pe.wait_ge(xh_ready, c + 1)
                    for t in range(TC):
                        last = nc.tensor.transpose(bank[:, P * t:P * (t + 1)], xh[:, c % 2, t, P * f:P * (f + 1)],
                                                   id_f[:, :])
                elif item[0] == "QK":
                    _, c, f, side = item
                    if part == 0:
                        pe.wait_ge(pro_done, 1 + PRO.index(("T", c, 1)))
                    last = nc.tensor.matmul(bank, (wq, wk)[side][:, part, P * f:P * (f + 1)],
                                            xT[:, part, CW * c:CW * (c + 1)], start=(part == 0), stop=(part == 1))
                else:
                    if n == PRO.index(("V", 0)) and part == 0:
                        pe.wait_ge(v_loaded, 16)
                    if part == 0:
                        pe.wait_ge(pro_done, 1 + PRO.index(("T", 2 * item[1] // TC, 1)))
                    kt = 2 * item[1] + part
                    for a in range(FC):
                        last = nc.tensor.matmul(bank[:, D * part:D * (part + 1)], xT[:, a, P * kt:P * (kt + 1)],
                                                wv[:, a, :], start=(a == 0), stop=(a == FC - 1))
                if part == BANK_PARTS[item[0]] - 1:
                    last.then_inc(pro_ready, 1)

            pe.sem_inc(pv_done, P_SLOTS)
            pe.wait_ge(id_loaded, 16)
            n = turns = 0
            for item, part in PLAN:
                if item[0] != "M":
                    if item == ("QK", 0, 0, 0) and part == 0:
                        pe.wait_ge(w_loaded, 64)
                    pro_bank(n, item, part)
                    n += part == BANK_PARTS[item[0]] - 1
                    continue
                i = item[1]
                if i == 0:
                    pe.wait_ge(consts_ready, 2)
                if i in M_CHUNK_START:
                    pe.wait_ge(first_ops[M_CHUNK_START.index(i)], 16 * 2 * len(RUNS))
                stream_entry(i, 0, i, turns)
                turns += STREAM[i][0] == "turn"

            for c in range(NC):
                if M_CHUNK_START[c] >= LEAD:
                    pe.wait_ge(first_ops[c], 16 * 2 * len(RUNS))
            pe.wait_ge(pro_done, len(PRO))

            def project(c):
                pe.wait_ge(at_ready, c + 1)
                if c == 0:
                    pe.wait_ge(m_done, SN * NG + 1)
                    pe.wait_ge(e_loaded, 16 * (3 + E))
                else:
                    pe.wait_ge(xt2_ready, 2 * c)
                for h in range(2):
                    for t in range(2):
                        tok = P * (2 * h + t)
                        for a in range(FC):
                            last = nc.tensor.matmul(PB[h][:, D * t:D * (t + 1)], at[:, a, tok:tok + P], wo[:, a, :],
                                                    start=(a == 0), stop=(a == FC - 1))
                    last.then_inc(wo_ready, 1)

            def turn(c):
                pe.wait_ge(xh2_ready, c + 1)
                for f in range(FC):
                    if f == 0 and c > 0:
                        pe.wait_ge(gt_ready, c)
                    for t in range(TC):
                        last = nc.tensor.transpose(XB[f][:, P * t:P * (t + 1)], xh2[:, t, P * f:P * (f + 1)], id_f[:, :])
                    last.then_inc(xt2_psum, 1)

            def logits(c):
                pe.wait_ge(xt2_ready, 2 * (c + 1))
                for t in range(TC):
                    for a in range(FC):
                        last = nc.tensor.matmul(MB[0][:, E * t:E * (t + 1)], xT2[:, c % 2, a, P * t:P * (t + 1)],
                                                wr_sb[:, a, :], start=(a == 0), stop=(a == FC - 1))
                last.then_inc(lg_ready, 1)

            def experts(c, t):
                for e2 in range(E // 2):
                    n = (TC * c + t) * (E // 2) + e2
                    if n >= 4:
                        pe.wait_ge(ex_done, n - 3)
                    elif n == 0:
                        pe.wait_ge(exp_done, 2 + NG * SS * 2)
                    for a in range(FC):
                        last = nc.tensor.matmul(ring4[n % 4], xT2[:, c % 2, a, P * t:P * (t + 1)],
                                                we_sb[:, a, 2 * F * e2:2 * F * (e2 + 1)],
                                                start=(a == 0), stop=(a == FC - 1))
                    last.then_inc(ex_ready, 1)

            def gate_turn(c):
                pe.wait_ge(gates_ready, c + 1)
                for t in range(TC):
                    last = nc.tensor.transpose(MB[0][0:E, P * t:P * (t + 1)], gates[:, c % 2, t, :], id_f[:, :])
                last.then_inc(gt_psum, 1)

            def gated_bias(c, h):
                if c == 0 and h == 0:
                    pe.wait_ge(o_out, NG * NC + 1)
                else:
                    pe.wait_ge(yb_ready, 2 * c + h)
                pe.wait_ge(gt_ready, c + 1)
                for t in range(2):
                    tok = P * (2 * h + t)
                    last = nc.tensor.matmul(OB[:, D * t:D * (t + 1)], gT[:, tok:tok + P], be_sb[:, :],
                                            start=True, stop=True)
                last.then_inc(gb_ready, 1)

            def group(pair, u, last=False):
                g = 2 * pair + u
                m_base = LEAD + SN * g

                def scores(s, j):
                    c, kt = STEPS[s]
                    w = CW - step_off(s)
                    if kt == 0 and j == 0:
                        slot = (c + 1) % 2
                        pe.wait_ge(mrow[slot], 48 * (2 * g + (c // 2 + 1)))
                    p = j // 2
                    if j % 2 == 0:
                        pe.wait_ge(exp_done, g * (2 * SS) + (2 * s + p + 1))
                    ins = nc.tensor.matmul(ST[p][:, j % 2, 0:w], Ko[u][0:SX, kt // TC, j, P * (kt % TC):P * (kt % TC + 1)],
                                           Qo[u][0:SX, c, j, CW - w:CW], start=True, stop=True)
                    if j % 2:
                        ins.then_inc(st_ready, 1)

                def values(s):
                    c, kt = STEPS[s]
                    w = CW - step_off(s)
                    if kt == 0:
                        pe.wait_ge(o_out, g * NC + (c + 1))
                    if diag(s) is None:
                        pe.wait_ge(exp_done, g * (2 * SS) + (2 * s + 2 + 2))
                    else:
                        pe.wait_ge(mask_done, g * DIAGS + (TC * c + diag(s) + 1))
                    for j in range(HG):
                        last = nc.tensor.matmul(
                            OB[32 * j:32 * j + VW, CW - w:CW], Vg[u][:, kt, j, :],
                            probs[:, s % P_SLOTS, j, 0:w], start=(kt == 0), stop=(kt == TC * (c + 1) - 1),
                            tile_position=(0, 32 * j))
                    last.then_inc(pv_done, 1)

                pe.wait_ge(vg_ready, g + 1)
                pe.wait_ge(ones_placed[u], 16)
                for s in range(SS):
                    mine = (LAST_BODY if last else BODY)[s]
                    between = [[] for _ in range(HG + 1)]
                    for k, entry in enumerate(mine):
                        between[(2 * k + 1) * (HG + 1) // (2 * len(mine))].append(entry)
                    for j in range(HG + 1):
                        if j < HG:
                            scores(s, j)
                        elif s >= PV_LAG:
                            values(s - PV_LAG)
                        for entry in between[j]:
                            i, following = entry
                            if following and i == 0:
                                pe.wait_ge(ops_loaded[1 - u], (pair + 1) * (16 * (TERMS + len(RUNS))))
                            stream_entry(i, 1 - u if following and not last else u, m_base + m_place(entry, last),
                                         NC * g + turn_number(entry), SN % M_RING if last and following else None)
                    if last:
                        if s == PROJECT_STEP:
                            project(0)
                        if s == TURN_STEP:
                            turn(0)
                        if s == LOGITS_STEP:
                            logits(0)
                for s in range(SS - PV_LAG, SS):
                    values(s)

            with pe.Fori(0, NG // 2 - 1) as it:
                for u in range(2):
                    group(it, u)
            group(NG // 2 - 1, 0)
            group(NG // 2 - 1, 1, last=True)

            for c in range(NC):
                more = c + 1 < NC
                experts(c, 0)
                if more:
                    project(c + 1)
                gate_turn(c)
                experts(c, 1)
                gated_bias(c, 0)
                if more:
                    turn(c + 1)
                experts(c, 2)
                if more:
                    logits(c + 1)
                experts(c, 3)
                gated_bias(c, 1)

        @block.scalar
        def _(act):
            act.sem_inc(exp_done, 2)
            act.sem_inc(o_out, 1)
            act.wait_ge(w_loaded, 64)
            nc.scalar.activation(bqk_half[:, :, :], bqk[:, :, :], ACT.Copy, scale=0.5).then_inc(bias_ready, 1)
            act.wait_ge(bias_ready, 1)
            v = 0
            pending = None

            def middle(v):
                act.wait_ge(rest_ready, v + 1)
                nc.scalar.activation(parts[:, v % 2, 1, :], r1[:, v % 2, :], ACT.Copy).then_inc(mid_ready, 1)

            for n, item in enumerate(PRO):
                act.wait_ge(pro_ready, n + 1)
                bank = ring4[n % 4]
                if item[0] == "T":
                    _, c, f = item
                    nc.scalar.activation(xT[:, f, CW * c:CW * (c + 1)], bank, ACT.Copy).then_inc(pro_done, 1)
                elif item[0] == "V":
                    kt = 2 * item[1]
                    nc.scalar.activation(V[:, kt:kt + 2, :].rearrange("p t d -> p (t d)"), bank, ACT.Copy)\
                      .then_inc(pro_done, 1)
                else:
                    _, c, f, side = item
                    if v >= 2:
                        act.wait_ge(rest_ready, v - 1)
                        for half in range(2):
                            act.wait_ge(parts_stored[v % 2][half], 16 * (v // 2))
                    nc.scalar.activation(qf[:, v % 2, :], bank, ACT.Identity, bias=bqk_half[:, side, f:f + 1],
                                         scale=0.5).then_inc(pro_done, 1)
                    act.wait_ge(pro_done, n + 1)
                    nc.scalar.activation(parts[:, v % 2, 0, :], qf[:, v % 2, :], ACT.Copy).then_inc(high_ready, 1)
                    if v % 2:
                        middle(v - 1)
                        middle(v)
                    v += 1

            def read_out(c, g):
                act.wait_ge(pv_done, P_SLOTS + g * SS + (C_END[c] + 1))
                act.wait_ge(o_stored[c % 2], 16 + (2 * g + c // 2) * 16)
                nc.scalar.activation(O_sb[:, c % 2, :], OB[:, :], ACT.Copy).then_inc(o_out, 1)

            def read_turn(c):
                for f in range(FC):
                    act.wait_ge(xt2_psum, 2 * c + f + 1)
                    if c >= 2 and f == 0:
                        act.wait_ge(ex_ready, (c - 1) * TC * (E // 2))
                    nc.scalar.activation(xT2[:, c % 2, f, :], XB[f][:, :], ACT.Copy).then_inc(xt2_ready, 1)

            def gate_exp(c):
                act.wait_ge(gd_ready, c + 1)
                nc.scalar.activation(ge[:, :], gd[:, :], ACT.Exp).then_inc(ge_ready, 1)

            def read_gates(c):
                act.wait_ge(gt_psum, c + 1)
                if c >= 1:
                    act.wait_ge(gb_ready, 2 * c)
                nc.scalar.activation(gT[:, :], MB[0][0:E, :], ACT.Copy).then_inc(gt_ready, 1)

            def group(g, last=False):
                for s in range(SS):
                    w = CW - step_off(s)
                    for p in range(2):
                        act.wait_ge(st_ready, g * (2 * SS) + (2 * s + p + 1))
                        if p == 0:
                            act.wait_ge(pv_done, g * SS + (s + 1))
                        nc.scalar.activation(probs[:, s % P_SLOTS, 2 * p:2 * p + 2, 0:w], ST[p][:, :, 0:w], ACT.Exp)\
                          .then_inc(exp_done, 1)
                    for c in range(NC - 1):
                        if s == C_END[c] + PV_LAG:
                            read_out(c, g)
                    if last and s == TURN_STEP + 1:
                        read_turn(0)
                    if last and s == GATE_STEP:
                        gate_exp(0)
                read_out(NC - 1, g)

            with act.Fori(0, NG // 2 - 1) as it:
                for u in range(2):
                    group(2 * it + u)
            group(NG - 2)
            group(NG - 1, last=True)

            for c in range(NC):
                read_gates(c)
                if c + 1 < NC:
                    read_turn(c + 1)
                    gate_exp(c + 1)

        @block.vector
        def _(dve):
            steps = [0]

            def link(ins):
                steps[0] += 1
                ins.then_inc(ln_step, 1)
                dve.wait_ge(ln_step, steps[0])

            def moments(n, tile):
                for t in range(TC):
                    last = nc.vector.bn_stats(st6[:, t, :], tile(t))
                    if t < TC - 1:
                        steps[0] += 1
                        last.then_inc(ln_step, 1)
                link(last)
                for t in range(TC):
                    last = nc.vector.bn_aggr(mv[:, n % 2, t, :], st6[:, t, :])
                    if t < TC - 1:
                        steps[0] += 1
                        last.then_inc(ln_step, 1)
                link(last)
                nc.vector.tensor_scalar(ve[:, n % 2, :], mv[:, n % 2, :, 1], EPS, None, ALU.add).then_inc(var_ready, 1)

            def scale(n, tile, put, done):
                dve.wait_ge(var_ready, n + 1)
                dve.wait_ge(rsqrt_ready, n + 1)
                r = rs[:, n % 2, :]
                link(nc.vector.scalar_tensor_tensor(ta[:, :], r, -0.5, r, ALU.mult, ALU.mult))
                link(nc.vector.tensor_tensor(tb[:, :], ta[:, :], ve[:, n % 2, :], ALU.mult))
                link(nc.vector.scalar_tensor_tensor(ta[:, :], tb[:, :], 1.5, r, ALU.add, ALU.mult))
                for t in range(TC):
                    last = nc.vector.tensor_scalar(put(t), tile(t), mv[:, n % 2, t, 0:1], ta[:, t:t + 1],
                                                   ALU.subtract, ALU.mult)
                    if t < TC - 1:
                        steps[0] += 1
                        last.then_inc(ln_step, 1)
                last.then_inc(done, 1)

            def stream_entry(i, n, mrow_seen, ring=None):
                m = STREAM[i]
                ring = i % M_RING if ring is None else ring
                bank = MB[ring]
                dve.wait_ge(m_ready, n + 1)
                if m[0] == "turn":
                    slot = (m[1] + 1) % 2
                    if mrow_seen is not None:
                        dve.wait_ge(mrow[slot], mrow_seen)
                    nc.vector.tensor_copy(mT[:, slot, :], bank[0:3 * HG * TC, 0:P // 2].bitcast(BF16))\
                      .then_inc(m_done, 1)
                    return
                _, c, t, j, kc = m
                w = m_width(m)
                if kc < c:
                    nc.vector.tensor_reduce(pm[:, c, TC * j + t, kc:kc + 1], bank[:, 0:w], AX.X, ALU.max)\
                      .then_inc(m_done, 1)
                else:
                    if not (isinstance(n, int) and n < M_RING):
                        dve.wait_ge(m_done, n + 1 - m_free(i))
                    dve.sem_inc(dve_passed, 1)
                    nc.vector.tensor_tensor_reduce(
                        out=junk[:, i % M_RING, 0:w], in0=bank[:, 0:w], in1=tri[:, CW - w:CW], scale=1.0, scalar=NEG,
                        op0=ALU.add, op1=ALU.max, accum_out=pm[:, c, TC * j + t, kc:kc + 1]).then_inc(m_done, 1)

            def fold(c, n):
                dve.wait_ge(m_done, n + 1)
                nc.vector.tensor_reduce(mr[:, :], pm[:, c, :, :], AX.X, ALU.max, negate=True).then_inc(folded, 1)

            def x_moments(c):
                dve.wait_ge(x_loaded[c], 16)
                moments(c, lambda t: x_sb[:, TC * c + t, :])

            x_moments(0)
            for c in range(NC):
                if c >= 1:
                    dve.wait_ge(xh_ready, c)
                if c + 1 < NC:
                    x_moments(c + 1)
                if c >= 2:
                    dve.wait_ge(pro_ready, 1 + PRO.index(("T", c - 2, 1)))
                scale(c, lambda t: x_sb[:, TC * c + t, :], lambda t: xh[:, c % 2, t, :], xh_ready)
            dve.wait_ge(id_loaded, 16)
            nc.vector.tensor_copy(id_b[:, :], id_f[:, :]).then_inc(consts_ready, 1)
            nc.vector.memset(mparts[:, :, :, :], 0.0).then_inc(consts_ready, 1)
            link(nc.vector.memset(pm[:, :, :, :], NEG))
            dve.wait_ge(tri_loaded, 16)
            for i in range(LEAD):
                stream_entry(i, i, None)
                if i in M_END:
                    fold(M_END.index(i), i)

            def invert(c):
                dve.wait_ge(den_loaded[c], 16)
                nc.vector.reciprocal(rden_c[:, DW * c:DW * (c + 1)], den_c[:, DW * c:DW * (c + 1)])\
                  .then_inc(rden_ready, 1)

            def attn(c):
                dve.wait_ge(at_loaded[c % 2], 16 * 2 * FC * (c // 2 + 1))
                if c >= 1:
                    dve.wait_ge(wo_ready, 2 * c)
                nc.vector.tensor_tensor(at[:, :, :], nm[:, c % 2, :, :], rd[:, c % 2, :, :], ALU.mult)\
                  .then_inc(at_ready, 1)

            def residual(c):
                for h in range(2):
                    dve.wait_ge(wo_ready, 2 * c + h + 1)
                    rows = x_sb[:, TC * c + 2 * h:TC * c + 2 * h + 2, :].rearrange("p t d -> p (t d)")
                    nc.vector.tensor_tensor(rows, PB[h][:, :], rows, ALU.add).then_inc(x1_ready, 1)
                dve.wait_ge(x1_ready, 2 * (c + 1))
                if c >= 1:
                    dve.wait_ge(xt2_psum, 2 * c)
                moments(NC + c, lambda t: x_sb[:, TC * c + t, :])
                scale(NC + c, lambda t: x_sb[:, TC * c + t, :], lambda t: xh2[:, t, :], xh2_ready)

            def route(c):
                dve.wait_ge(lg_ready, c + 1)
                nc.vector.tensor_copy(lg[:, :, :], MB[0][:, 0:TC * E].rearrange("p (t e) -> p t e", e=E))\
                  .then_inc(lg_read, 1)
                dve.wait_ge(lg_read, c + 1)
                for t in range(TC):
                    link(nc.vector.max(top[:, t, :], lg[:, t, :]))
                for t in range(TC):
                    link(nc.vector.max_index(idx[:, t, :], top[:, t, :], lg[:, t, :]))
                nc.vector.tensor_tensor(gd[:, :], top[:, :, 1], top[:, :, 0], ALU.subtract).then_inc(gd_ready, 1)
                link(nc.vector.tensor_copy(idf[:, :, :], idx[:, :, 0:2]))
                dve.wait_ge(ge_ready, c + 1)
                link(nc.vector.tensor_scalar(gs[:, :], ge[:, :], 1.0, None, ALU.add))
                link(nc.vector.reciprocal(gw[:, :, 0], gs[:, :]))
                link(nc.vector.tensor_tensor(gw[:, :, 1], gw[:, :, 0], ge[:, :], ALU.mult))
                for t in range(TC):
                    for n, dst in ((0, g1), (1, g2)):
                        steps[0] += 1
                        nc.vector.tensor_scalar(dst[:, t, :], iota[:, :], idf[:, t, n:n + 1], gw[:, t, n:n + 1],
                                                ALU.is_equal, ALU.mult).then_inc(ln_step, 1)
                dve.wait_ge(ln_step, steps[0])
                nc.vector.tensor_tensor(gates[:, c % 2, :, :], g1[:, :, :], g2[:, :, :], ALU.add)\
                  .then_inc(gates_ready, 1)
                dve.wait_ge(gates_ready, c + 1)

            def combine(c, t):
                if c >= 2 and t == 0:
                    dve.wait_ge(y_stored[c % 2], 16 * 2 * (c // 2))
                y = yb[:, c % 2, t, :]
                for e2 in range(E // 2):
                    n = (TC * c + t) * (E // 2) + e2
                    dve.wait_ge(ex_ready, n + 1)
                    for h in range(2):
                        e = 2 * e2 + h
                        ins = nc.vector.scalar_tensor_tensor(
                            out=y, in0=ring4[n % 4][:, F * h:F * (h + 1)], scalar=gates[:, c % 2, t, e:e + 1],
                            in1=x_sb[:, TC * c + t, :] if e == 0 else y, op0=ALU.mult, op1=ALU.add)
                        if h == 0:
                            link(ins)
                        else:
                            ins.then_inc(ex_done, 1)
                            dve.wait_ge(ex_done, n + 1)

            def add_bias(c, h):
                dve.wait_ge(gb_ready, 2 * c + h + 1)
                y = yb[:, c % 2, 2 * h:2 * h + 2, :].rearrange("p t d -> p (t d)")
                nc.vector.tensor_tensor(y, OB[:, :], y, ALU.add).then_inc(yb_ready, 1)

            def group(g, last=False):
                m_base = LEAD + SN * g
                for s in range(SS):
                    for entry in (LAST_BODY if last else BODY)[s]:
                        i, following = entry
                        number = m_base + m_place(entry, last)
                        seen = None
                        if STREAM[i][0] == "turn":
                            c = STREAM[i][1]
                            uses = {2: 1, 3: 1, 0: 2, 1: 2}[c]
                            seen = 48 * (2 * g + uses)
                        stream_entry(i, number, seen, SN % M_RING if last and following else None)
                        if i in M_END:
                            fold(M_END.index(i), number)
                    if last and s in RDEN_STEP[:2]:
                        invert(RDEN_STEP.index(s))

            with dve.Fori(0, NG // 2 - 1) as it:
                for u in range(2):
                    group(2 * it + u)
            group(NG - 2)
            group(NG - 1, last=True)

            attn(0)
            dve.wait_ge(xb_ready, NC)
            residual(0)
            attn(1)
            invert(2)
            dve.wait_ge(iota_ready, E)
            route(0)
            for c in range(NC):
                more = c + 1 < NC
                combine(c, 0)
                if more:
                    residual(c + 1)
                combine(c, 1)
                if c == 0:
                    invert(NC - 1)
                if c + 2 < NC:
                    attn(c + 2)
                add_bias(c, 0)
                combine(c, 2)
                if more:
                    route(c + 1)
                combine(c, 3)
                add_bias(c, 1)

        @block.gpsimd
        def _(pool):
            steps = [0]

            def link(ins):
                steps[0] += 1
                ins.then_inc(vg_set, 1)
                pool.wait_ge(vg_set, steps[0])

            def split_maxima(c, number):
                split = mparts[:, (c + 1) % 2, :, :]
                pool.wait_ge(folded, number)

                pool.sem_inc(pool_passed, 1)

                def step(k, ins):
                    ins.then_inc(mpost_step, 1)
                    pool.wait_ge(mpost_step, (number - 1) * 3 + k)
                    pool.sem_inc(pool_passed, 1)

                step(1, nc.gpsimd.tensor_copy(split[:, 0, :], mr[:, :]))
                step(2, nc.gpsimd.tensor_tensor(mx[:, :], mr[:, :], split[:, 0, :], ALU.subtract))
                step(3, nc.gpsimd.tensor_copy(split[:, 1, :], mx[:, :]))
                nc.gpsimd.tensor_tensor(split[:, 2, :], mx[:, :], split[:, 1, :], ALU.subtract)\
                    .then_inc(mparts_ready, 1)

            def split_pair(v):
                for k in (v, v + 1):
                    pool.wait_ge(high_ready, k + 1)
                    nc.gpsimd.tensor_tensor(r1[:, k % 2, :], qf[:, k % 2, :], parts[:, k % 2, 0, :], ALU.subtract)\
                        .then_inc(rest_ready, 1)
                for k in (v, v + 1):
                    pool.wait_ge(mid_ready, k + 1)
                    nc.gpsimd.tensor_tensor(parts[:, k % 2, 2, :], r1[:, k % 2, :], parts[:, k % 2, 1, :],
                                            ALU.subtract).then_inc(low_ready, 1)

            def place_values(b, col):
                src = V[:, :, bass.ds(col, HG * DH)].rearrange("p k (j d) -> p k j d", d=DH)
                bias = bv_sb[:, bass.ds(col, HG * DH)].rearrange("p (j d) -> p j d", d=DH)\
                    .unsqueeze(1).broadcast_to([P, NT, HG, DH])
                pool.sem_inc(pool_passed, 1)
                nc.gpsimd.tensor_tensor(Vg[b][:, :, :, 0:DH], src, bias, ALU.add).then_inc(vg_ready, 1)

            link(nc.gpsimd.memset(neg_half[:, :], -0.5))
            for b in range(2):
                link(nc.gpsimd.memset(Vg[b][:, :, :, DH:VW], 0.0))
                link(nc.gpsimd.memset(Vg[b][:, :, :, DH:DH + 1], 1.0))
            nc.gpsimd.memset(ones[:, :], 1.0).then_inc(ones_ready, 1)

            def rsqrt(n):
                pool.wait_ge(var_ready, n + 1)
                nc.gpsimd.tensor_tensor(rs[:, n % 2, :], ve[:, n % 2, :], neg_half[:, :], ALU.pow)\
                    .then_inc(rsqrt_ready, 1)

            for c in range(NC):
                rsqrt(c)
            v = maxima = 0
            for item in DONE:
                if item[0] == "QK" and item[3] == 1:
                    split_pair(v)
                    v += 2
                elif item == ("V", NT // 2 - 1):
                    pool.wait_ge(biases_loaded, 32)
                    pool.wait_ge(pro_done, 1 + PRO.index(item))
                    place_values(0, 0)
                elif item[0] == "M" and item[1] in M_END:
                    maxima += 1
                    split_maxima(M_END.index(item[1]), maxima)

            def group(g, u, last=False):
                pool.wait_ge(pv_done, P_SLOTS + SS * g)
                if not last:
                    pool.sem_inc(pool_passed, 1)
                    place_values(1 - u, (g + 1) * (HG * DH))
                for s in range(SS):
                    c, _ = STEPS[s]
                    if diag(s) is not None:
                        pool.wait_ge(exp_done, g * (2 * SS) + (2 * s + 4))
                        pool.sem_inc(pool_passed, 1)
                        block_ = probs[:, s % P_SLOTS, :, 0:P]
                        nc.gpsimd.affine_select(out=block_, in_=block_, compare_op=ALU.is_ge, fill=0.0, base=0,
                                                pattern=[[0, HG], [1, P]], channel_multiplier=-1)\
                            .then_inc(mask_done, 1)
                    for entry in (LAST_BODY if last else BODY)[s]:
                        if entry[0] in M_END:
                            split_maxima(M_END.index(entry[0]), NC * g + turn_number(entry))
                    if last and s == XB_STEP:
                        project_bias()
                    if last and s == PROJECT_STEP:
                        rsqrt(NC)

            def project_bias():
                pool.wait_ge(xh_ready, NC)
                for c in range(NC):
                    rows = x_sb[:, TC * c:TC * (c + 1), :]
                    nc.gpsimd.tensor_tensor(rows, rows, bo_sb[:, :].unsqueeze(1).broadcast_to([P, TC, D]), ALU.add)\
                        .then_inc(xb_ready, 1)
                for e in range(E):
                    nc.gpsimd.memset(iota[:, e:e + 1], float(e)).then_inc(iota_ready, 1)

            with pool.Fori(0, NG // 2 - 1) as it:
                for u in range(2):
                    group(2 * it + u, u)
            group(NG - 2, 0)
            group(NG - 1, 1, last=True)

            for c in range(1, NC):
                rsqrt(NC + c)


def kernel(L0_attn_X, L0_attn_Wq, L0_attn_bq, L0_attn_Wk, L0_attn_bk, L0_attn_Wv, L0_attn_bv, L0_attn_Wo, L0_attn_bo,
           L0_ffn_Wr, L0_ffn_We, L0_ffn_be):
    import numpy as np
    import concourse.bacc as bacc
    from concourse.bass_utils import run_bass_kernel_spmd

    def lay(a):
        return np.ascontiguousarray(a)

    def by_group(a):
        a = np.asarray(a)
        return lay(np.swapaxes(a.reshape(a.shape[:-1] + (NG, HG, DH)), -1, -2).reshape(a.shape))

    arrays = {
        "X": lay(np.asarray(L0_attn_X).reshape(S, D)),
        "WqT": by_group(np.asarray(L0_attn_Wq).T), "WkT": by_group(np.asarray(L0_attn_Wk).T),
        "WvT": lay(np.asarray(L0_attn_Wv).T), "WoT": lay(np.asarray(L0_attn_Wo).T),
        "bq": by_group(L0_attn_bq), "bk": by_group(L0_attn_bk), "bv": lay(L0_attn_bv), "bo": lay(L0_attn_bo),
        "Wr": lay(L0_ffn_Wr), "We": lay(L0_ffn_We), "be": lay(L0_ffn_be),
        "ident": np.eye(P, dtype=np.float32),
        "trimask": np.where(np.arange(CW)[None, :] - (CW - P) <= np.arange(P)[:, None], 0.0, NEG).astype(np.float32),
    }
    nc = bacc.Bacc("TRN2", target_bir_lowering=False, num_devices=1)
    args, feed = {}, {}
    for name, a in arrays.items():
        feed["in_" + name] = a
        args[name] = nc.dram_tensor("in_" + name, a.shape, mybir.dt.from_np(a.dtype), kind="ExternalInput").ap()
    shape, dtype = (S, D), np.dtype("float32")
    out = nc.dram_tensor("out_y", shape, mybir.dt.from_np(dtype), kind="ExternalOutput").ap()
    build_program(nc, out=out, **args)
    r = run_bass_kernel_spmd(nc, [feed], core_ids=[0])
    return r.results[0]["out_y"].reshape(1, S, D)
```
